# Optimizing a Trainium2 kernel written in Bass

```python
import numpy as np
import jax
import jax.numpy as jnp

def _softmax(x, axis=-1):
    return jax.nn.softmax(x, axis=axis)

def _gelu(x):
    return jax.nn.gelu(x, approximate=True)

def _silu(x):
    return jax.nn.silu(x)

def _sigmoid(x):
    return jax.nn.sigmoid(x)

def _layernorm(x, axis=-1, eps=1e-05):
    m = jnp.mean(x, axis=axis, keepdims=True)
    v = jnp.var(x, axis=axis, keepdims=True)
    return (x - m) / jnp.sqrt(v + eps)

def _scatter_add(tgt, idx, src, axis=0):
    return tgt.at[idx].add(src)

def _segment_sum(src, seg, n):
    return jax.ops.segment_sum(src, seg, n)
kernel_name = 'mk_adaln_d1_jaxref_r4_d89538'

def setup_inputs(seed: int=0):
    np.random.seed(seed)
    _w = jnp.asarray

    def _L0_attn_setup():
        import jax, jax.numpy as jnp
        import numpy as np
        D_MODEL = 256
        N_HEADS = 16
        HEAD_DIM = D_MODEL // N_HEADS
        D_FF = 1024
        WINDOW = 128
        LN_EPS = 1e-05
        NEG_INF = jnp.finfo(jnp.float32).min

        def layer_norm(x, w, b):
            mu = jnp.mean(x, axis=-1, keepdims=True)
            var = jnp.mean(jnp.square(x - mu), axis=-1, keepdims=True)
            return (x - mu) * jax.lax.rsqrt(var + LN_EPS) * w + b
        key = jax.random.key(seed)
        ks = jax.random.split(key, 12)
        B, L, D = (2, 512, D_MODEL)
        s = 1.0 / np.sqrt(D)
        inp = {'x': jax.random.normal(ks[0], (B, L, D), jnp.float32), 'Wq': jax.random.normal(ks[1], (D, D), jnp.float32) * s, 'bq': jnp.zeros((D,), jnp.float32), 'Wk': jax.random.normal(ks[2], (D, D), jnp.float32) * s, 'bk': jnp.zeros((D,), jnp.float32), 'Wv': jax.random.normal(ks[3], (D, D), jnp.float32) * s, 'bv': jnp.zeros((D,), jnp.float32), 'Wo': jax.random.normal(ks[4], (D, D), jnp.float32) * s, 'bo': jnp.zeros((D,), jnp.float32), 'W1': jax.random.normal(ks[5], (D, D_FF), jnp.float32) * s, 'b1': jnp.zeros((D_FF,), jnp.float32), 'W2': jax.random.normal(ks[6], (D_FF, D), jnp.float32) * (1.0 / np.sqrt(D_FF)), 'b2': jnp.zeros((D,), jnp.float32), 'ln1_w': jnp.ones((D,), jnp.float32), 'ln1_b': jnp.zeros((D,), jnp.float32), 'ln2_w': jnp.ones((D,), jnp.float32), 'ln2_b': jnp.zeros((D,), jnp.float32)}
        return inp
    _L0_attn_in = _L0_attn_setup()

    def _L0_ffn_setup():
        import jax, jax.numpy as jnp
        import numpy as np
        DIM = 256

        def _reference_tuple_inner(x, W_r, W_k, W_v, mu_r, mu_k):
            B, T, C = x.shape
            x_prev = jnp.concatenate([jnp.zeros((B, 1, C), x.dtype), x[:, :-1, :]], axis=1)
            xr = mu_r * x + (1.0 - mu_r) * x_prev
            xk = mu_k * x + (1.0 - mu_k) * x_prev
            r = jax.nn.sigmoid(jnp.einsum('btc,dc->btd', xr, W_r))
            k = jnp.einsum('btc,dc->btd', xk, W_k)
            k_act = jnp.square(jax.nn.relu(k))
            out = r * jnp.einsum('btc,dc->btd', k_act, W_v)
            new_state = x[:, -1, :]
            return (out, new_state)
        key = jax.random.key(seed)
        ks = jax.random.split(key, 6)
        B, T, C = (8, 512, DIM)
        x = jax.random.normal(ks[0], (B, T, C), dtype=jnp.float32)
        s = 1.0 / np.sqrt(C)
        W_r = jax.random.uniform(ks[1], (C, C), jnp.float32, -s, s)
        W_k = jax.random.uniform(ks[2], (C, C), jnp.float32, -s, s)
        W_v = jax.random.uniform(ks[3], (C, C), jnp.float32, -s, s)
        mu_r = jax.random.uniform(ks[4], (C,), jnp.float32)
        mu_k = jax.random.uniform(ks[5], (C,), jnp.float32)
        return {'x': x, 'W_r': W_r, 'W_k': W_k, 'W_v': W_v, 'mu_r': mu_r, 'mu_k': mu_k}
    _L0_ffn_in = _L0_ffn_setup()
    _L0_c = _w((lambda *s: np.random.randn(*s).astype(np.float32) * 0.05)(8, 256))
    _L0_wmod = _w((lambda *s: np.random.randn(*s).astype(np.float32) * 0.05)(256, 6 * 256) * 256 ** (-0.5))
    _d = {'L0_attn_x': _L0_attn_in['x'], 'L0_attn_Wq': _L0_attn_in['Wq'], 'L0_attn_bq': _L0_attn_in['bq'], 'L0_attn_Wk': _L0_attn_in['Wk'], 'L0_attn_bk': _L0_attn_in['bk'], 'L0_attn_Wv': _L0_attn_in['Wv'], 'L0_attn_bv': _L0_attn_in['bv'], 'L0_attn_Wo': _L0_attn_in['Wo'], 'L0_attn_bo': _L0_attn_in['bo'], 'L0_attn_W1': _L0_attn_in['W1'], 'L0_attn_b1': _L0_attn_in['b1'], 'L0_attn_W2': _L0_attn_in['W2'], 'L0_attn_b2': _L0_attn_in['b2'], 'L0_attn_ln1_w': _L0_attn_in['ln1_w'], 'L0_attn_ln1_b': _L0_attn_in['ln1_b'], 'L0_attn_ln2_w': _L0_attn_in['ln2_w'], 'L0_attn_ln2_b': _L0_attn_in['ln2_b'], 'L0_ffn_W_r': _L0_ffn_in['W_r'], 'L0_ffn_W_k': _L0_ffn_in['W_k'], 'L0_ffn_W_v': _L0_ffn_in['W_v'], 'L0_ffn_mu_r': _L0_ffn_in['mu_r'], 'L0_ffn_mu_k': _L0_ffn_in['mu_k'], 'L0_c': _L0_c, 'L0_wmod': _L0_wmod}
    _x0 = _d['L0_attn_x']
    _d['L0_attn_x'] = jax.random.normal(jax.random.fold_in(jax.random.key(seed), 1), (8, 512, 256), dtype=_x0.dtype)
    del _x0
    return _d

def reference(L0_attn_x, L0_attn_Wq, L0_attn_bq, L0_attn_Wk, L0_attn_bk, L0_attn_Wv, L0_attn_bv, L0_attn_Wo, L0_attn_bo, L0_attn_W1, L0_attn_b1, L0_attn_W2, L0_attn_b2, L0_attn_ln1_w, L0_attn_ln1_b, L0_attn_ln2_w, L0_attn_ln2_b, L0_ffn_W_r, L0_ffn_W_k, L0_ffn_W_v, L0_ffn_mu_r, L0_ffn_mu_k, L0_c, L0_wmod):

    def _L0_attn_ref(x, Wq, bq, Wk, bk, Wv, bv, Wo, bo, W1, b1, W2, b2, ln1_w, ln1_b, ln2_w, ln2_b):
        import jax, jax.numpy as jnp
        import numpy as np
        D_MODEL = 256
        N_HEADS = 16
        HEAD_DIM = D_MODEL // N_HEADS
        D_FF = 1024
        WINDOW = 128
        LN_EPS = 1e-05
        NEG_INF = jnp.finfo(jnp.float32).min

        def layer_norm(x, w, b):
            mu = jnp.mean(x, axis=-1, keepdims=True)
            var = jnp.mean(jnp.square(x - mu), axis=-1, keepdims=True)
            return (x - mu) * jax.lax.rsqrt(var + LN_EPS) * w + b
        B, L, D = x.shape
        i = jnp.arange(L)[:, None]
        j = jnp.arange(L)[None, :]
        band = (j > i) | (i - j > WINDOW)
        bias = jnp.where(band, NEG_INF, 0.0).astype(x.dtype)
        h = layer_norm(x, ln1_w, ln1_b)
        q = (h @ Wq + bq).reshape(B, L, N_HEADS, HEAD_DIM)
        k = (h @ Wk + bk).reshape(B, L, N_HEADS, HEAD_DIM)
        v = (h @ Wv + bv).reshape(B, L, N_HEADS, HEAD_DIM)
        scale = 1.0 / np.sqrt(HEAD_DIM)
        scores = jnp.einsum('blhd,bmhd->bhlm', q, k) * scale + bias
        attn = jax.nn.softmax(scores, axis=-1)
        ctx = jnp.einsum('bhlm,bmhd->blhd', attn, v).reshape(B, L, D)
        x = x + ctx @ Wo + bo
        h2 = layer_norm(x, ln2_w, ln2_b)
        x = x + jax.nn.gelu(h2 @ W1 + b1) @ W2 + b2
        return x

    def _L0_ffn_ref(x, W_r, W_k, W_v, mu_r, mu_k):
        import jax, jax.numpy as jnp
        import numpy as np
        DIM = 256

        def _reference_tuple_inner(x, W_r, W_k, W_v, mu_r, mu_k):
            B, T, C = x.shape
            x_prev = jnp.concatenate([jnp.zeros((B, 1, C), x.dtype), x[:, :-1, :]], axis=1)
            xr = mu_r * x + (1.0 - mu_r) * x_prev
            xk = mu_k * x + (1.0 - mu_k) * x_prev
            r = jax.nn.sigmoid(jnp.einsum('btc,dc->btd', xr, W_r))
            k = jnp.einsum('btc,dc->btd', xk, W_k)
            k_act = jnp.square(jax.nn.relu(k))
            out = r * jnp.einsum('btc,dc->btd', k_act, W_v)
            new_state = x[:, -1, :]
            return (out, new_state)
        return _reference_tuple_inner(x, W_r, W_k, W_v, mu_r, mu_k)[0]
    x = L0_attn_x
    mod = (_silu(L0_c) @ L0_wmod).reshape(L0_c.shape[0], 6, 1, -1)
    sa, ca, ga, sb, cb, gb = (mod[:, 0], mod[:, 1], mod[:, 2], mod[:, 3], mod[:, 4], mod[:, 5])
    ga = (2 * (ga >= 0) - 1) * jnp.maximum(jnp.abs(ga), 0.25)
    gb = (2 * (gb >= 0) - 1) * jnp.maximum(jnp.abs(gb), 0.25)
    h = _layernorm(x, axis=-1) * (1 + ca) + sa
    x = x + ga * _L0_attn_ref(h, L0_attn_Wq, L0_attn_bq, L0_attn_Wk, L0_attn_bk, L0_attn_Wv, L0_attn_bv, L0_attn_Wo, L0_attn_bo, L0_attn_W1, L0_attn_b1, L0_attn_W2, L0_attn_b2, L0_attn_ln1_w, L0_attn_ln1_b, L0_attn_ln2_w, L0_attn_ln2_b)
    h = _layernorm(x, axis=-1) * (1 + cb) + sb
    x = x + gb * _L0_ffn_ref(h, L0_ffn_W_r, L0_ffn_W_k, L0_ffn_W_v, L0_ffn_mu_r, L0_ffn_mu_k)
    return x

_drawn_inputs = setup_inputs


def setup_inputs(seed=0):
    import zlib

    import numpy as np

    out = dict(_drawn_inputs(seed))
    spreads = {'L0_attn_bq': (0.0, 0.8),
     'L0_attn_bk': (0.0, 2.0),
     'L0_attn_bv': (0.0, 0.374),
     'L0_attn_bo': (0.0, 0.284),
     'L0_attn_b1': (0.0, 0.51),
     'L0_attn_b2': (0.0, 0.307),
     'L0_attn_ln1_w': (1.0, 0.6),
     'L0_attn_ln1_b': (0.0, 0.282),
     'L0_attn_ln2_w': (1.0, 0.2),
     'L0_attn_ln2_b': (0.0, 0.493)}
    factors = {'L0_ffn_W_r': 8.0,
     'L0_ffn_W_k': 3.135,
     'L0_ffn_W_v': 2.859,
     'L0_ffn_mu_r': 8.0,
     'L0_ffn_mu_k': 5.168}
    for name, (base, spread) in spreads.items():
        noise = np.random.default_rng([zlib.crc32(name.encode()), seed]).standard_normal(out[name].shape)
        drawn = base * np.exp(spread * noise) if base else spread * noise
        out[name] = jnp.asarray(drawn.astype(out[name].dtype))
    for name, factor in factors.items():
        out[name] = (out[name] * factor).astype(out[name].dtype)
    return out
```

```python
from contextlib import ExitStack

import concourse.bass as bass
from concourse import mybir

F32 = mybir.dt.float32
F32R = mybir.dt.float32r
BF16 = mybir.dt.bfloat16
F16 = mybir.dt.float16
ALU = mybir.AluOpType
ACT = mybir.ActivationFunctionType
AX = mybir.AxisListType

P = 128
NEG = -3.0e38
EPS = 1e-5
DMA = 16


class Signal:

    def __init__(self, sem, unit=1):
        self.sem, self.unit, self.per = sem, unit, 0


class Ring:

    def __init__(self, banks):
        self.banks, self.uses = banks, []

    def take(self):
        use = {"bank": self.banks[len(self.uses) % len(self.banks)], "n": len(self.uses), "free": None}
        self.uses.append(use)
        return use

    def before(self, use):
        k = len(self.banks)
        if use["n"] >= k:
            return (*self.uses[use["n"] - k]["free"], 0)
        assert len(self.uses) % k == 0
        return (*self.uses[len(self.uses) - k + use["n"]]["free"], 1)


def wait(eng, signal, n, b):
    per, unit = signal.per, signal.unit
    if isinstance(b, int):
        if b >= 0 and b * per + n > 0:
            eng.wait_ge(signal.sem, (b * per + n) * unit)
    else:
        eng.wait_ge(signal.sem, b * (per * unit) + n * unit)


class Plan:

    def __init__(self):
        self.steps = []

    def do(self, engine, emit, waits=(), signal=None, cost=0, gate=None):
        n = 0
        if signal is not None:
            signal.per += 1
            n = signal.per

        def run(eng, b):
            for w in waits:
                w = w() if callable(w) else w
                s, count, back = w if len(w) == 3 else (*w, 0)
                wait(eng, s, s.per if count is None else count, b - back if back else b)
            if gate is not None and not isinstance(b, int):
                eng.sem_inc(gate, 1)
            last = emit(eng, b)
            if signal is not None:
                last.then_inc(signal.sem, signal.unit)

        self.steps.append((engine, run, cost))
        return n


def merged(*parts):
    keyed = []
    for which, (steps, offset) in enumerate(parts):
        total = sum(c for _, _, c in steps) or 1
        done = 0
        for k, (engine, run, cost) in enumerate(steps):
            keyed.append((done / total, which, k, engine, run, offset))
            done += cost
    keyed.sort(key=lambda x: x[:3])
    return [(engine, run, offset) for _, _, _, engine, run, offset in keyed]


def adaln_block(nc, x, w_attn, w_ff1, w_ff2, w_mix, w_mod, c_t, cols, bo, b2, out):
    B, L, D = x.shape
    NT = L // P
    KC = D // P
    FF = w_ff1.shape[1]
    MF = FF // P
    H = 16
    HD = D // H
    HS = H // 2
    VW = 3 * HD + 1
    SCALE = float(HD) ** -0.5
    PW = 2 * L - P
    MROW = 3 * HD

    ctx = ExitStack()
    with ctx:
        def sb(name, shape, dt=F32):
            return ctx.enter_context(nc.sbuf_tensor(name, shape, dt))

        def sem(name):
            return ctx.enter_context(nc.semaphore(name))

        def sig(name, unit=1):
            return Signal(sem(name), unit)

        scratch = nc.dram_tensor("mod_rows", (B, 4, D), F32, kind="Internal").ap()

        wa_hi, wa_lo = sb("wa_hi", [P, KC, 4 * D], F32R), sb("wa_lo", [P, KC, 4 * D], F32R)
        w1_hi, w1_lo = sb("w1_hi", [P, KC, FF], F32R), sb("w1_lo", [P, KC, FF], F32R)
        wb_hi, wb_lo = sb("wb_hi", [P, KC, 3 * D], F32R), sb("wb_lo", [P, KC, 3 * D], F32R)
        w2_sb = sb("w2_sb", [P, MF, D])
        ident = sb("ident", [P, P])
        ident_b = sb("ident_b", [P, P], BF16)
        mask = sb("mask", [P, 6, P], BF16)
        mhalf = sb("mhalf", [P, NT])
        col = sb("col", [P, cols.shape[1]])
        bias_q = sb("bias_q", [P, 4])
        bias_1 = sb("bias_1", [P, MF])
        cv = sb("cv", [P, KC])
        ct = sb("ct", [P, KC, B])
        sct = sb("sct", [P, KC, B])
        mod_t = sb("mod_t", [P, B, 4])
        mod_c = sb("mod_c", [P, 4])
        row_o = sb("row_o", [P, D])
        row_2 = sb("row_2", [P, D])
        xa = sb("xa", [P, NT, D])
        mod_a = sb("mod_a", [P, 2, D])
        h = sb("h", [P, NT, D])
        hn = sb("hn", [P, NT, D])
        st_a, mv_a = sb("st_a", [P, NT, 6]), sb("mv_a", [P, NT, 2])
        ve_a, rs_a = sb("ve_a", [P, NT]), sb("rs_a", [P, NT])
        at_hi, at_lo = sb("at_hi", [P, KC, L], F32R), sb("at_lo", [P, KC, L], F32R)
        qk_hi, qk_lo = sb("qk_hi", [P, 2, L], F32R), sb("qk_lo", [P, 2, L], F32R)
        q_st = sb("q_st", [P, HS, L], F32R)
        k_st = sb("k_st", [P, 2, HS, L], F32R)
        v_sb = sb("v_sb", [P, NT * H, VW], BF16)
        nmax = sb("nmax", [P, NT, H])
        nm_hl = sb("nm_hl", [P, NT, 2, H], F32R)
        m_t = sb("m_t", [2 * H, L], F32R)
        p32 = [sb(f"p32_{i}", [P, PW]) for i in range(2)]
        p_hi = [sb(f"p_hi{i}", [P, PW], F16) for i in range(2)]
        p_lo = [sb(f"p_lo{i}", [P, PW], F16) for i in range(2)]
        rsum = sb("rsum", [P, 2, 2 * NT])
        csum = sb("csum", [P, 2, 2 * NT, HD])
        x1 = sb("x1", [P, NT, D])
        x2 = sb("x2", [P, NT, D])
        mod_b = sb("mod_b", [P, 2, D])
        n2 = sb("n2", [P, NT, D])
        st_b, mv_b = sb("st_b", [P, NT, 6]), sb("mv_b", [P, NT, 2])
        ve_b, rs_b = sb("ve_b", [P, NT]), sb("rs_b", [P, NT])
        bt_hi, bt_lo = sb("bt_hi", [P, KC, L], F32R), sb("bt_lo", [P, KC, L], F32R)
        kt_hi, kt_lo = sb("kt_hi", [P, KC, L], F32R), sb("kt_lo", [P, KC, L], F32R)
        g = sb("g", [P, MF * L + KC])
        hid = g[:, 0:MF * L].rearrange("p (m n) -> p m n", m=MF)
        xrk = g[:, 0:KC * L].rearrange("p (k n) -> p k n", k=KC)
        dif = g[:, 2 * L:4 * L].rearrange("p (k n) -> p k n", k=KC)
        tr = g[:, 4 * L:6 * L].rearrange("p (t n) -> p t n", t=NT)
        h3 = g[:, 6 * L:8 * L + KC].rearrange("p (k n) -> p k n", k=KC)

        psum = [ctx.enter_context(nc.psum_tensor(f"bank{i}", [P, 512], F32)) for i in range(8)]
        ring_s = Ring(psum[0:2])
        ring_t = Ring(psum[2:4])
        ring_c = Ring(psum[4:6])
        ring_b = Ring(psum[6:8])

        c_ln1w, c_ln1b, c_ln2w, c_ln2b, c_bq, c_bv, c_b1, c_mur, c_muk = 0, 2, 4, 6, 8, 12, 14, 22, 24

        x_t = x.rearrange("b (t p) c -> b p t c", p=P)
        out_t = out.rearrange("b (t p) c -> b p t c", p=P)

        s_pool, s_dve = sem("s_pool"), sem("s_dve")

        tick_v, tick_p = sem("tick_v"), sem("tick_p")

        A1, A2 = Plan(), Plan()
        B1, B2 = Plan(), Plan()
        x_in, moda_in = sig("x_in", DMA), sig("moda_in", DMA)
        st0, mv0, ve0, rs0 = sig("st0"), sig("mv0"), sig("ve0"), sig("rs0")
        hpre, hfull = sig("hpre"), sig("hfull")
        st1, mv1, ve1, rs1, hn_s = sig("st1"), sig("mv1"), sig("ve1"), sig("rs1"), sig("hn")
        h_row = sig("h_row")
        tr1, at1_hi, at1_lo = sig("tr1"), sig("at1_hi"), sig("at1_lo")
        qk_mm, qk_h, qk_l = sig("qk_mm"), sig("qk_h"), sig("qk_l")
        stack = [sig(f"stack{m}", DMA) for m in range(4)]
        zero_in, max_in = sig("zero_in", DMA), sig("max_in", DMA)
        v_mm, v1_s, vr_s, v2_s, v3_s = sig("v_mm"), sig("v1"), sig("vr"), sig("v2"), sig("v3")
        s_mm, s_max = sig("s_mm"), sig("s_max")
        nm_hi_s, nm_lo_s, mt_tr, mt_s = sig("nm_hi"), sig("nm_lo"), sig("mt_tr"), sig("mt")
        st_mm, exp_s, sel_s, ph_s = sig("st_mm"), sig("exp"), sig("sel"), sig("p_hi")
        pl_v, pl_g = sig("pl_v"), sig("pl_g")
        av_mm, rcp_s, cs_s, ctx_s = sig("av_mm"), sig("rcp"), sig("csum"), sig("ctx")
        ctr, at2_hi, at2_lo = sig("ctr"), sig("at2_hi"), sig("at2_lo")
        wo_mm, x1_s = sig("wo_mm"), sig("x1")
        x_in_b, modb_in = sig("x_in_b", DMA), sig("modb_in", DMA)
        st2, mv2, ve2, rs2, n2_s = sig("st2"), sig("mv2"), sig("ve2"), sig("rs2"), sig("n2")
        x1_row = sig("x1_row")
        tr2, bt1_hi, bt1_lo = sig("tr2"), sig("bt1_hi"), sig("bt1_lo")
        f1_mm, gelu_s, f2_mm, y_s, yg_s, x2_s = sig("f1_mm"), sig("gelu"), sig("f2_mm"), sig("y"), sig("yg"), sig("x2")
        st3, mv3, ve3, rs3, n3_s = sig("st3"), sig("mv3"), sig("ve3"), sig("rs3"), sig("n3")
        modc_s, zcol = sig("modc"), sig("zcol")
        tr3, h3_s, dif_s = sig("tr3"), sig("h3"), sig("dif")
        xr_s, xr_h, xr_l = sig("xr"), sig("xr_h"), sig("xr_l")
        xk_s, xk_h, xk_l = sig("xk"), sig("xk_h"), sig("xk_l")
        r_mm, r_s, k_mm, relu_s, ksq_s, ka_h, ka_l = (sig(n) for n in ("r_mm", "r", "k_mm", "relu", "ksq", "ka_h", "ka_l"))
        vb_mm, o1_s, o2_s, o3_s, out_s = sig("vb_mm"), sig("o1"), sig("o2"), sig("o3"), sig("out_s", DMA)

        def norm_stats(plan, src, st, mv, ve, rs, s_st, s_mv, s_ve, s_rs, ready, free):
            for t in range(NT):
                plan.do("vector", lambda e, b, t=t: e.bn_stats(st[:, t, :], src[:, t, :]),
                        ready(t) + [free], s_st)
            for t in range(NT):
                plan.do("vector", lambda e, b, t=t: e.bn_aggr(mv[:, t, :], st[:, t, :]),
                        [lambda t=t: (s_st, t + 1)] + [free], s_mv, gate=tick_v)
            plan.do("gpsimd", lambda e, b: e.tensor_scalar(ve[:, :], mv[:, :, 1], 1.0, EPS, ALU.mult, ALU.add),
                    [(s_mv, None)], s_ve, gate=tick_p)
            plan.do("gpsimd", lambda e, b: e.tensor_tensor(rs[:, :], ve[:, :], mhalf[:, :], ALU.pow),
                    [(s_ve, None)], s_rs)

        def transposes(plan, ring, src, k, waits, signal):
            use = ring.take()

            def emit(e, b):
                for t in range(NT):
                    last = e.transpose(use["bank"][:, t * P:(t + 1) * P], src[:, t, k * P:(k + 1) * P], ident[:, :])
                return last
            n = plan.do("tensor", emit, waits + [lambda: ring.before(use)], signal, 4 * 60)
            return use, n

        def three(e, dst, a_hi, a_lo, b_hi, b_lo):
            for k in range(KC):
                e.matmul(dst, a_hi(k), b_hi(k), start=(k == 0), stop=False)
                e.matmul(dst, a_hi(k), b_lo(k), start=False, stop=False)
                last = e.matmul(dst, a_lo(k), b_hi(k), start=False, stop=(k == KC - 1))
            return last

        A1.do("sync", lambda e, b: e.dma_start(xa[:, :, :], x_t[b] if isinstance(b, int) else x_t[bass.ds(b, 1)].rearrange("o p t c -> (o p) t c")),
              [(hpre, None, 1)], x_in)
        A1.do("sync", lambda e, b: e.dma_start(mod_a[:, :, :], mod_bcast(b, 0)), [(hfull, None, 1)], moda_in)

        def mod_bcast(b, r):
            s = scratch[b if isinstance(b, int) else bass.ds(b, 1), r:r + 2, :]
            if isinstance(b, int):
                s = s.rearrange("(o r) c -> o r c", o=1)
            return s.broadcast_to([P, 2, D])

        norm_stats(A1, xa, st_a, mv_a, ve_a, rs_a, st0, mv0, ve0, rs0, lambda t: [(x_in, 1)], (hn_s, None, 1))
        for t in range(NT):
            A1.do("vector", lambda e, b, t=t: e.scalar_tensor_tensor(
                out=h[:, t, :], in0=xa[:, t, :], scalar=mv_a[:, t, 0:1], in1=mod_a[:, 0, :],
                op0=ALU.subtract, op1=ALU.mult), [(mv0, NT), (moda_in, 1), (x1_s, None, 1)], hpre)
        for t in range(NT):
            A1.do("vector", lambda e, b, t=t: e.scalar_tensor_tensor(
                out=h[:, t, :], in0=h[:, t, :], scalar=rs_a[:, t:t + 1], in1=mod_a[:, 1, :],
                op0=ALU.mult, op1=ALU.add), [(rs0, 1), (hpre, t + 1)], hfull)
        norm_stats(A1, h, st_a, mv_a, ve_a, rs_a, st1, mv1, ve1, rs1, lambda t: [(hfull, t + 1), (mv0, t + 1)], (hfull, NT))
        for t in range(NT):
            A1.do("vector", lambda e, b, t=t: e.tensor_scalar(
                hn[:, t, :], h[:, t, :], mv_a[:, t, 0:1], rs_a[:, t:t + 1], ALU.subtract, ALU.mult),
                [(rs1, 1), (ctr, None, 1)], hn_s)
        A1.do("gpsimd", lambda e, b: e.tensor_tensor(
            h[:, :, :], h[:, :, :], row_o[:, :].rearrange("p (o c) -> p o c", o=1).broadcast_to([P, NT, D]), ALU.add),
            [(hn_s, NT)], h_row)
        for k in range(KC):
            use, n = transposes(A1, ring_s, hn, k, [(hn_s, NT)], tr1)
            A1.do("scalar", lambda e, b, k=k, use=use: e.activation(at_hi[:, k, :], use["bank"][:, :], ACT.Copy),
                  [(tr1, n), (wo_mm, None, 1)], at1_hi)
            m = A1.do("vector", lambda e, b, k=k, use=use: e.tensor_tensor(
                at_lo[:, k, :], use["bank"][:, :], at_hi[:, k, :].bitcast(F32), ALU.subtract),
                [(at1_hi, k + 1), (wo_mm, None, 1)], at1_lo)
            use["free"] = (at1_lo, m)
        A1.do("sync", lambda e, b: e.dma_start(q_st[MROW:MROW + 2, :, :].bitcast(F32), k_st[64:64 + 2, 0, :, :].bitcast(F32)),
              [(st_mm, None, 1)], zero_in)
        A1.do("sync", lambda e, b: e.dma_start(q_st[64 + MROW:64 + MROW + 2, :, :].bitcast(F32), k_st[64:64 + 2, 0, :, :].bitcast(F32)),
              [], zero_in)
        for m in range(4):
            is_k, half = m % 2, m // 2
            c0 = is_k * D + half * P
            use = ring_s.take()
            slot = m % 2
            A1.do("tensor", lambda e, b, c0=c0, use=use: three(
                e, use["bank"][:, :], lambda k: wa_hi[:, k, c0:c0 + P], lambda k: wa_lo[:, k, c0:c0 + P],
                lambda k: at_hi[:, k, :], lambda k: at_lo[:, k, :]),
                [(at1_lo, KC), lambda use=use: ring_s.before(use)], qk_mm, 6 * 216)
            bias = bias_q[:, 2 * is_k + half:2 * is_k + half + 1]
            free = (stack[m - 2], 3) if m >= 2 else (stack[m + 2], None, 1)
            A1.do("scalar", lambda e, b, use=use, slot=slot, bias=bias: e.activation(
                qk_hi[:, slot, :], use["bank"][:, :], ACT.Identity, bias=bias), [(qk_mm, m + 1), free], qk_h)
            n = A1.do("vector", lambda e, b, use=use, slot=slot, bias=bias: e.scalar_tensor_tensor(
                out=qk_lo[:, slot, :], in0=use["bank"][:, :], scalar=bias, in1=qk_hi[:, slot, :].bitcast(F32),
                op0=ALU.add, op1=ALU.subtract), [(qk_h, m + 1), free], qk_l)
            use["free"] = (qk_l, n)
            src = [qk_hi, qk_hi, qk_lo] if is_k else [qk_hi, qk_lo, qk_hi]
            for j in range(3):
                r0 = 64 * half + HD * j
                dst = k_st[r0:r0 + HD, half, :, :] if is_k else q_st[r0:r0 + HD, :, :]
                A1.do("sync", lambda e, b, dst=dst, s=src[j], slot=slot: e.dma_start(dst.bitcast(F32), s[:, slot, :].bitcast(F32)),
                      [(qk_l, m + 1), (st_mm, None, 1)] if j == 0 else [], stack[m])
        for t2 in range(NT // 2):
            use = ring_s.take()

            def emit(e, b, t2=t2, use=use):
                for t in (2 * t2, 2 * t2 + 1):
                    last = three(e, use["bank"][:, (t % 2) * D:(t % 2) * D + D],
                                 lambda k: at_hi[:, k, t * P:(t + 1) * P], lambda k: at_lo[:, k, t * P:(t + 1) * P],
                                 lambda k: wa_hi[:, k, 2 * D:3 * D], lambda k: wa_lo[:, k, 2 * D:3 * D])
                return last
            A1.do("tensor", emit, [lambda use=use: ring_s.before(use)], v_mm, 12 * 109)
            rows = slice(2 * t2 * H, (2 * t2 + 2) * H)
            bank = use["bank"][:, :].rearrange("p (u d) -> p u d", d=HD)
            rest = hn[:, 2 * t2:2 * t2 + 2, :].rearrange("p t (u d) -> p (t u) d", d=HD)
            A1.do("scalar", lambda e, b, rows=rows, bank=bank: e.activation(v_sb[:, rows, 0:HD], bank, ACT.Copy),
                  [(v_mm, t2 + 1), (av_mm, None, 1)], v1_s)
            n = A1.do("vector", lambda e, b, rows=rows, bank=bank, rest=rest: e.tensor_tensor(
                rest, bank, v_sb[:, rows, 0:HD], ALU.subtract), [(v1_s, t2 + 1), (tr1, KC)], vr_s)
            use["free"] = (vr_s, n)
            A1.do("scalar", lambda e, b, rows=rows, rest=rest: e.activation(v_sb[:, rows, HD:2 * HD], rest, ACT.Copy),
                  [(vr_s, t2 + 1)], v2_s)
            A1.do("vector", lambda e, b, rows=rows, rest=rest: e.tensor_tensor(
                v_sb[:, rows, 2 * HD:3 * HD], rest, v_sb[:, rows, HD:2 * HD], ALU.subtract),
                [(v2_s, t2 + 1)], v3_s)
        for hd in range(H):
            half, j = hd // HS, hd % HS
            for q2 in range(NT // 2):
                use = ring_s.take()

                def emit(e, b, half=half, j=j, q2=q2, use=use):
                    e.matmul(use["bank"][:, :], ident_b[:, :], mask[:, 2 * q2:2 * q2 + 4, :].rearrange("p a c -> p (a c)"),
                             start=True, stop=False)
                    for qt in (2 * q2, 2 * q2 + 1):
                        lo = max(qt - 1, 0) * P
                        c1 = (qt % 2 + 1) * 2 * P
                        last = e.matmul(use["bank"][:, c1 - ((qt + 1) * P - lo):c1], q_st[:, j, qt * P:(qt + 1) * P],
                                        k_st[:, half, j, lo:(qt + 1) * P], start=False, stop=(qt % 2 == 1))
                    return last
                w = [(stack[m], 3) for m in range(4)] + [(zero_in, 2)] if hd == 0 and q2 == 0 else []
                A1.do("tensor", emit, w + [lambda use=use: ring_s.before(use)], s_mm, 434)
                n = A1.do("vector", lambda e, b, hd=hd, q2=q2, use=use: e.tensor_reduce(
                    nmax[:, 2 * q2:2 * q2 + 2, hd], use["bank"][:, :].rearrange("p (t k) -> p t k", t=2),
                    AX.X, ALU.max, negate=True), [(s_mm, 2 * hd + q2 + 1), (nm_lo_s, None, 1)], s_max)
                use["free"] = (s_max, n)
        A1.do("vector", lambda e, b: e.tensor_copy(nm_hl[:, :, 0, :], nmax[:, :, :]), [(s_max, None), (mt_tr, None, 1)], nm_hi_s)
        A1.do("vector", lambda e, b: e.tensor_tensor(nm_hl[:, :, 1, :], nmax[:, :, :], nm_hl[:, :, 0, :].bitcast(F32), ALU.subtract),
              [(nm_hi_s, 1)], nm_lo_s)
        for t2 in range(NT // 2):
            use = ring_s.take()

            def emit(e, b, t2=t2, use=use):
                for t in range(2):
                    last = e.transpose(use["bank"][0:2 * H, t * P:(t + 1) * P],
                                       nm_hl[:, 2 * t2 + t, :, :].rearrange("p a c -> p (a c)").bitcast(F32), ident[:, :])
                return last
            A1.do("tensor", emit, [(nm_lo_s, 1), lambda use=use: ring_s.before(use)], mt_tr, 120)
            n = A1.do("vector", lambda e, b, t2=t2, use=use: e.tensor_copy(
                m_t[:, 2 * t2 * P:(2 * t2 + 2) * P], use["bank"][0:2 * H, 0:2 * P]),
                [(mt_tr, t2 + 1), (max_in, None, 1)], mt_s)
            use["free"] = (mt_s, n)
        for half in range(2):
            for part in range(2):
                r0, s0 = 64 * half + MROW + part, part * H + half * HS
                A1.do("sync", lambda e, b, r0=r0, s0=s0: e.dma_start(q_st[r0:r0 + 1, :, :].bitcast(F32), m_t[s0:s0 + HS, :].bitcast(F32)),
                      [(mt_s, None), (s_mm, None)] if half == part == 0 else [], max_in)

        def scores_t(hd):
            half, j, slot = hd // HS, hd % HS, hd % 2
            for k2 in range(NT // 2):
                use = ring_t.take()

                def emit(e, b, use=use, k2=k2):
                    for kt in (2 * k2, 2 * k2 + 1):
                        n = min(2 * P, L - kt * P)
                        c0 = (kt % 2) * 2 * P
                        last = e.matmul(use["bank"][:, c0:c0 + n], k_st[:, half, j, kt * P:(kt + 1) * P],
                                        q_st[:, j, kt * P:kt * P + n], start=True, stop=True)
                    return last
                A2.do("tensor", emit, ([(max_in, 4)] if hd == 0 and k2 == 0 else []) + [lambda use=use: ring_t.before(use)],
                      st_mm, 218 if k2 == 0 else 165)
                c0, n = k2 * 4 * P, min(4 * P, PW - k2 * 4 * P)
                w = [(st_mm, 2 * hd + k2 + 1)]
                w += [last_lo(hd - 2)] if hd >= 2 else [(*last_lo_of(H - 2 + slot), 1)]
                m = A2.do("scalar", lambda e, b, use=use, c0=c0, n=n, slot=slot: e.activation(
                    p32[slot][:, c0:c0 + n], use["bank"][:, 0:n], ACT.Exp, scale=SCALE), w, exp_s)
                use["free"] = (exp_s, m)
            A2.do("gpsimd", lambda e, b, slot=slot: e.affine_select(
                out=blocks(p32[slot], 0), in_=blocks(p32[slot], 0), compare_op=ALU.is_ge, fill=0.0, base=0,
                pattern=[[0, NT - 1], [1, P]], channel_multiplier=-1), [(exp_s, 2 * hd + 2)], sel_s, gate=tick_p)
            A2.do("gpsimd", lambda e, b, slot=slot: e.affine_select(
                out=p32[slot][:, PW - P:PW], in_=p32[slot][:, PW - P:PW], compare_op=ALU.is_ge, fill=0.0, base=0,
                pattern=[[1, P]], channel_multiplier=-1), [], sel_s)
            A2.do("gpsimd", lambda e, b, slot=slot: e.affine_select(
                out=blocks(p32[slot], 1), in_=blocks(p32[slot], 1), compare_op=ALU.is_ge, fill=0.0, base=0,
                pattern=[[0, NT - 1], [-1, P]], channel_multiplier=1), [], sel_s)
            free = [(av_mm, hd - 1)] if hd >= 2 else [(av_mm, H - 1 + slot, 1)]
            A2.do("scalar", lambda e, b, slot=slot: e.activation(p_hi[slot][:, :], p32[slot][:, :], ACT.Copy),
                  [(sel_s, 3 * hd + 3)] + free, ph_s)
            A2.do("gpsimd" if on_pool(hd) else "vector", lambda e, b, slot=slot: e.tensor_tensor(
                p_lo[slot][:, :], p32[slot][:, :], p_hi[slot][:, :], ALU.subtract),
                [(ph_s, hd + 1)] + free, pl_g if on_pool(hd) else pl_v)

        def blocks(tile, k):
            return tile[:, 0:(NT - 1) * 2 * P].rearrange("p (t c) -> p t c", t=NT - 1)[:, :, k * P:(k + 1) * P]

        def on_pool(hd):
            return hd % 3 == 2

        def last_lo_of(hd):
            same = [i for i in range(hd + 1) if on_pool(i) == on_pool(hd)]
            return (pl_g if on_pool(hd) else pl_v, len(same))

        last_lo = last_lo_of
        uses_c = {}

        def context(hd):
            slot, pair = hd % 2, hd // 2
            if hd % 2 == 0:
                uses_c[pair] = ring_c.take()
            use = uses_c[pair]

            def emit(e, b):
                for qt in range(NT):
                    u = (hd % 2) * NT + qt
                    dst = use["bank"][:, u * VW:(u + 1) * VW]
                    pieces = [(pt[slot], kt, qt - kt) for pt in (p_hi, p_lo) for kt in range(max(qt - 1, 0), qt + 1)]
                    for i, (pt, kt, k) in enumerate(pieces):
                        c0 = kt * 2 * P + k * P
                        last = e.matmul(dst, pt[:, c0:c0 + P], v_sb[:, kt * H + hd, :],
                                        start=(i == 0), stop=(i == len(pieces) - 1))
                return last
            w = [last_lo_of(hd)] + ([lambda use=use: ring_c.before(use)] if hd % 2 == 0 else [])
            A2.do("tensor", emit, w + ([(v3_s, None)] if hd == 0 else []), av_mm, 14 * 35)
            if hd % 2 == 0:
                return
            s2 = pair % 2
            bank = use["bank"][:, 0:2 * NT * VW].rearrange("p (u w) -> p u w", w=VW)
            A2.do("vector", lambda e, b: e.reciprocal(rsum[:, s2, :], bank[:, :, VW - 1]),
                  [(av_mm, hd + 1), (ctx_s, pair - 1) if pair >= 2 else (ctx_s, H // 2 - 1 + pair, 1)], rcp_s)
            n = A2.do("vector", lambda e, b: e.tensor_reduce(
                csum[:, s2, :, :], bank[:, :, 0:3 * HD].rearrange("p u (s d) -> p u d s", s=3), AX.X, ALU.add),
                [], cs_s)
            use["free"] = (cs_s, n)
            dst = hn[:, :, (hd - 1) * HD:(hd + 1) * HD].rearrange("p t (u d) -> p u t d", u=2)
            A2.do("vector", lambda e, b: e.tensor_tensor(
                dst, csum[:, s2, :, :].rearrange("p (u t) d -> p u t d", u=2),
                rsum[:, s2, :].rearrange("p (u t o) -> p u t o", u=2, o=1).broadcast_to([P, 2, NT, HD]), ALU.mult),
                [(cs_s, pair + 1), (v3_s, None)], ctx_s)

        for hd in range(H + 1):
            if hd < H:
                scores_t(hd)
            if hd >= 1:
                context(hd - 1)
        for k in range(KC):
            use, n = transposes(A2, ring_s, hn, k, [(ctx_s, None)], ctr)
            A2.do("scalar", lambda e, b, k=k, use=use: e.activation(at_hi[:, k, :], use["bank"][:, :], ACT.Copy),
                  [(ctr, n), (v_mm, None)], at2_hi)
            m = A2.do("vector", lambda e, b, k=k, use=use: e.tensor_tensor(
                at_lo[:, k, :], use["bank"][:, :], at_hi[:, k, :].bitcast(F32), ALU.subtract), [(at2_hi, k + 1)], at2_lo)
            use["free"] = (at2_lo, m)
        for t2 in range(NT // 2):
            use = ring_s.take()

            def emit(e, b, t2=t2, use=use):
                for t in (2 * t2, 2 * t2 + 1):
                    last = three(e, use["bank"][:, (t % 2) * D:(t % 2) * D + D],
                                 lambda k: at_hi[:, k, t * P:(t + 1) * P], lambda k: at_lo[:, k, t * P:(t + 1) * P],
                                 lambda k: wa_hi[:, k, 3 * D:4 * D], lambda k: wa_lo[:, k, 3 * D:4 * D])
                return last
            A2.do("tensor", emit, [(at2_lo, KC), lambda use=use: ring_s.before(use)], wo_mm, 12 * 109)
            n = A2.do("vector", lambda e, b, t2=t2, use=use: e.tensor_tensor(
                x1[:, 2 * t2:2 * t2 + 2, :], use["bank"][:, :].rearrange("p (t c) -> p t c", t=2),
                h[:, 2 * t2:2 * t2 + 2, :], ALU.add), [(wo_mm, t2 + 1), (h_row, 1), (x2_s, None, 1)], x1_s)
            use["free"] = (x1_s, n)
        if len(ring_s.uses) % 2:
            raise AssertionError(len(ring_s.uses))

        B1.do("sync", lambda e, b: e.dma_start(mod_b[:, :, :], mod_bcast(b, 2)), [(o2_s, None, 1)], modb_in)
        B1.do("sync", lambda e, b: e.dma_start(x2[:, :, :], x_t[b] if isinstance(b, int) else x_t[bass.ds(b, 1)].rearrange("o p t c -> (o p) t c")),
              [(out_s, None, 1)], x_in_b)
        B1.do("vector", lambda e, b: e.tensor_copy(mod_c[:, :], mod_t[:, b, :] if isinstance(b, int) else mod_t[:, bass.ds(b, 1), :].rearrange("p o f -> p (o f)")),
              [(h3_s, None, 1)], modc_s)
        norm_stats(B1, x1, st_b, mv_b, ve_b, rs_b, st2, mv2, ve2, rs2, lambda t: [(x1_s, None)], (n3_s, None, 1))
        for t in range(NT):
            B1.do("vector", lambda e, b, t=t: e.tensor_scalar(
                n2[:, t, :], x1[:, t, :], mv_b[:, t, 0:1], rs_b[:, t:t + 1], ALU.subtract, ALU.mult),
                [(rs2, 1), (tr3, None, 1)], n2_s)
        B1.do("gpsimd", lambda e, b: e.tensor_tensor(
            x1[:, :, :], x1[:, :, :], row_2[:, :].rearrange("p (o c) -> p o c", o=1).broadcast_to([P, NT, D]), ALU.add),
            [(n2_s, NT)], x1_row)
        for k in range(KC):
            use, n = transposes(B1, ring_b, n2, k, [(n2_s, NT)], tr2)
            B1.do("scalar", lambda e, b, k=k, use=use: e.activation(bt_hi[:, k, :], use["bank"][:, :], ACT.Copy),
                  [(tr2, n), (vb_mm, None, 1)], bt1_hi)
            m = B1.do("vector", lambda e, b, k=k, use=use: e.tensor_tensor(
                bt_lo[:, k, :], use["bank"][:, :], bt_hi[:, k, :].bitcast(F32), ALU.subtract),
                [(bt1_hi, k + 1), (vb_mm, None, 1)], bt1_lo)
            use["free"] = (bt1_lo, m)
        for m in range(MF):
            use = ring_b.take()
            B1.do("tensor", lambda e, b, m=m, use=use: three(
                e, use["bank"][:, :], lambda k: w1_hi[:, k, m * P:(m + 1) * P], lambda k: w1_lo[:, k, m * P:(m + 1) * P],
                lambda k: bt_hi[:, k, :], lambda k: bt_lo[:, k, :]),
                [(bt1_lo, KC), lambda use=use: ring_b.before(use)], f1_mm, 6 * 216)
            n = B1.do("scalar", lambda e, b, m=m, use=use: e.activation(
                hid[:, m, :], use["bank"][:, :], ACT.Gelu_apprx_tanh, bias=bias_1[:, m:m + 1]),
                [(f1_mm, m + 1), (o1_s, None, 1), (ksq_s, None, 1), (xk_l, None, 1)], gelu_s)
            use["free"] = (gelu_s, n)
        for t2 in range(NT // 2):
            use = ring_b.take()

            def emit(e, b, t2=t2, use=use):
                for t in (2 * t2, 2 * t2 + 1):
                    for m in range(MF):
                        last = e.matmul(use["bank"][:, (t % 2) * D:(t % 2) * D + D], hid[:, m, t * P:(t + 1) * P],
                                        w2_sb[:, m, :], start=(m == 0), stop=(m == MF - 1))
                return last
            B2.do("tensor", emit, [(gelu_s, MF), lambda use=use: ring_b.before(use)], f2_mm, 16 * 432)
            ts = slice(2 * t2, 2 * t2 + 2)
            n = B2.do("vector", lambda e, b, ts=ts, use=use: e.tensor_tensor(
                x1[:, ts, :], use["bank"][:, :].rearrange("p (t c) -> p t c", t=2), x1[:, ts, :], ALU.add),
                [(f2_mm, t2 + 1), (x1_row, 1)], y_s)
            use["free"] = (y_s, n)
            B2.do("gpsimd", lambda e, b, ts=ts: e.tensor_tensor(
                x1[:, ts, :], x1[:, ts, :], mod_b[:, 0:1, :].broadcast_to([P, 2, D]), ALU.mult),
                [(y_s, t2 + 1), (modb_in, 1)], yg_s)
            B2.do("vector", lambda e, b, ts=ts: e.tensor_tensor(
                x2[:, ts, :], x2[:, ts, :], x1[:, ts, :], ALU.add), [(yg_s, t2 + 1), (x_in_b, 1)], x2_s)
        norm_stats(B2, x2, st_b, mv_b, ve_b, rs_b, st3, mv3, ve3, rs3, lambda t: [(x2_s, t // 2 + 1), (mv2, t + 1)], (n2_s, NT))
        for t in range(NT):
            B2.do("vector", lambda e, b, t=t: e.tensor_scalar(
                n2[:, t, :], x2[:, t, :], mv_b[:, t, 0:1], rs_b[:, t:t + 1], ALU.subtract, ALU.mult),
                [(rs3, 1), (tr2, KC)], n3_s)
        B2.do("vector", lambda e, b: e.memset(h3[:, :, 0:1], 0.0), [(f2_mm, None)], zcol)
        for k in range(KC):
            use, n = transposes(B2, ring_b, n2, k, [(n3_s, NT)], tr3)
            m = B2.do("scalar", lambda e, b, k=k, use=use: e.activation(
                h3[:, k, 1:L + 1], use["bank"][:, :], ACT.Identity, bias=mod_c[:, k:k + 1], scale=mod_c[:, KC + k:KC + k + 1]),
                [(tr3, n), (modc_s, 1), (f2_mm, None)], h3_s)
            use["free"] = (h3_s, m)
        B2.do("gpsimd", lambda e, b: e.tensor_tensor(dif, h3[:, :, 1:L + 1], h3[:, :, 0:L], ALU.subtract),
              [(h3_s, KC), (zcol, 1), (f2_mm, None)], dif_s)
        for c_mu, s_x, s_h, s_l, hi, lo, free in ((c_mur, xr_s, xr_h, xr_l, bt_hi, bt_lo, (f1_mm, None)),
                                                  (c_muk, xk_s, xk_h, xk_l, kt_hi, kt_lo, (k_mm, None, 1))):
            for k in range(KC):
                w = [(dif_s, 1)] if s_x is xr_s else [(xr_l, k + 1)]
                B2.do("vector", lambda e, b, k=k, c_mu=c_mu: e.scalar_tensor_tensor(
                    out=xrk[:, k, :], in0=dif[:, k, :], scalar=col[:, c_mu + k:c_mu + k + 1], in1=h3[:, k, 0:L],
                    op0=ALU.mult, op1=ALU.add), w, s_x)
                B2.do("scalar", lambda e, b, k=k, hi=hi: e.activation(hi[:, k, :], xrk[:, k, :], ACT.Copy),
                      [(s_x, k + 1), free], s_h)
                B2.do("vector", lambda e, b, k=k, hi=hi, lo=lo: e.tensor_tensor(
                    lo[:, k, :], xrk[:, k, :], hi[:, k, :].bitcast(F32), ALU.subtract), [(s_h, k + 1), free], s_l)

        def token_rows(signal, waits, a_hi, a_lo, c0):
            uses = []
            for t2 in range(NT // 2):
                use = ring_b.take()

                def emit(e, b, t2=t2, use=use):
                    for t in (2 * t2, 2 * t2 + 1):
                        last = three(e, use["bank"][:, (t % 2) * D:(t % 2) * D + D],
                                     lambda k: a_hi[:, k, t * P:(t + 1) * P], lambda k: a_lo[:, k, t * P:(t + 1) * P],
                                     lambda k: wb_hi[:, k, c0:c0 + D], lambda k: wb_lo[:, k, c0:c0 + D])
                    return last
                B2.do("tensor", emit, waits + [lambda use=use: ring_b.before(use)], signal, 12 * 109)
                uses.append(use)
                yield t2, use

        for t2, use in token_rows(r_mm, [(xr_l, KC)], bt_hi, bt_lo, 0):
            n = B2.do("scalar", lambda e, b, t2=t2, use=use: e.activation(
                tr[:, 2 * t2:2 * t2 + 2, :], use["bank"][:, :].rearrange("p (t c) -> p t c", t=2), ACT.Tanh, scale=0.5),
                [(r_mm, t2 + 1), (f2_mm, None)], r_s)
            use["free"] = (r_s, n)
        for m in range(KC):
            use = ring_b.take()
            B2.do("tensor", lambda e, b, m=m, use=use: three(
                e, use["bank"][:, :], lambda k: wb_hi[:, k, D + m * P:D + (m + 1) * P], lambda k: wb_lo[:, k, D + m * P:D + (m + 1) * P],
                lambda k: kt_hi[:, k, :], lambda k: kt_lo[:, k, :]),
                [(xk_l, KC), lambda use=use: ring_b.before(use)], k_mm, 6 * 216)
            n = B2.do("scalar", lambda e, b, m=m, use=use: e.activation(xrk[:, m, :], use["bank"][:, :], ACT.Relu),
                      [(k_mm, m + 1), (xk_l, KC)], relu_s)
            use["free"] = (relu_s, n)
            B2.do("scalar", lambda e, b, m=m: e.activation(dif[:, m, :], xrk[:, m, :], ACT.Square),
                  [(relu_s, m + 1), (xk_s, KC)], ksq_s)
            B2.do("scalar", lambda e, b, m=m: e.activation(bt_hi[:, m, :], dif[:, m, :], ACT.Copy),
                  [(ksq_s, m + 1), (r_mm, None)], ka_h)
            B2.do("vector", lambda e, b, m=m: e.tensor_tensor(
                bt_lo[:, m, :], dif[:, m, :], bt_hi[:, m, :].bitcast(F32), ALU.subtract),
                [(ka_h, m + 1), (r_mm, None)], ka_l)
        for t2, use in token_rows(vb_mm, [(ka_l, KC)], bt_hi, bt_lo, 2 * D):
            ts = slice(2 * t2, 2 * t2 + 2)
            n = B2.do("vector", lambda e, b, ts=ts, use=use: e.scalar_tensor_tensor(
                out=tr[:, ts, :].rearrange("p t c -> p (t c)"), in0=tr[:, ts, :].rearrange("p t c -> p (t c)"), scalar=1.0,
                in1=use["bank"][:, :], op0=ALU.add, op1=ALU.mult),
                [(vb_mm, t2 + 1), (r_s, t2 + 1)], o1_s)
            use["free"] = (o1_s, n)
            B2.do("gpsimd", lambda e, b, ts=ts: e.tensor_tensor(
                tr[:, ts, :], tr[:, ts, :], mod_b[:, 1:2, :].broadcast_to([P, 2, D]), ALU.mult), [(o1_s, t2 + 1)], o2_s)
            B2.do("vector", lambda e, b, ts=ts: e.tensor_tensor(x2[:, ts, :], x2[:, ts, :], tr[:, ts, :], ALU.add),
                  [(o2_s, t2 + 1), (n3_s, NT)], o3_s)
        B2.do("sync", lambda e, b: e.dma_start(out_t[b] if isinstance(b, int) else out_t[bass.ds(b, 1)].rearrange("o p t c -> (o p) t c"), x2[:, :, :]),
              [(o3_s, None)], out_s)
        assert len(ring_b.uses) % 2 == 0 and len(ring_c.uses) % 2 == 0 and len(ring_t.uses) % 2 == 0

        first = merged((A1.steps, 0)) + merged((A2.steps, 0))
        body = merged((A1.steps, 0), (B1.steps, -1)) + merged((A2.steps, 0), (B2.steps, -1))
        final = merged((B1.steps, 0)) + merged((B2.steps, 0))

        def play(eng, name, order, b):
            for engine, run, offset in order:
                if engine == name:
                    run(eng, b + offset if offset else b)

        def batches(eng, name):
            play(eng, name, first, 0)
            play(eng, name, body, 1)
            with eng.Fori(2, B) as i:
                play(eng, name, body, i)
            play(eng, name, final, B - 1)

        s_col, s_ct, s_mod, s_rows = sem("s_col"), sem("s_ct"), sem("s_mod"), sem("s_rows")
        s_w = [sem(f"s_w{i}") for i in range(4)]
        s_act, s_pe = sem("s_act"), sem("s_pe")
        s_ones, s_scr, s_modrow = sem("s_ones"), sem("s_scr"), sem("s_modrow")
        mod_row = h[0:B, :, :]
        mod_x = p32[0][0:B, 0:2 * D].rearrange("b (r c) -> b r c", r=2)
        stage = [g[:, 0:8 * D], g[:, 8 * D:16 * D]]
        stage_a = stage[0].rearrange("p (k n) -> p k n", k=KC)
        stage_1 = stage[1].rearrange("p (k n) -> p k n", k=KC)
        stage_m = stage[0][:, 0:KC * 3 * D].rearrange("p (k n) -> p k n", k=KC)
        wmod = [x1, x2, n2]
        wmod_v = [t[:, :, :].rearrange("p (k a) c -> p k (a c)", k=KC) for t in wmod]
        pm = psum[0:3]
        pc = psum[3]
        pb = psum[5]
        pr = psum[4]

        block = ctx.enter_context(nc.Block())

        @block.sync
        def _(e):
            e.dma_start(col[:, :], cols).then_inc(s_col, DMA)
            e.dma_start(ct[:, :, :], c_t.rearrange("(k p) b -> p k b", p=P)).then_inc(s_ct, DMA)
            for i in range(3):
                e.dma_start(wmod_v[i], w_mod[:, i * 2 * D:(i + 1) * 2 * D].rearrange("(k p) n -> p k n", p=P)).then_inc(s_mod, DMA)
            e.dma_start(stage_a, w_attn.rearrange("(k p) n -> p k n", p=P)).then_inc(s_w[0], DMA)
            e.dma_start(row_o[:, :], bo.rearrange("(o c) -> o c", o=1).broadcast_to([P, D])).then_inc(s_rows, DMA)
            e.dma_start(row_2[:, :], b2.rearrange("(o c) -> o c", o=1).broadcast_to([P, D])).then_inc(s_rows, DMA)
            e.dma_start(stage_1, w_ff1.rearrange("(k p) n -> p k n", p=P)).then_inc(s_w[1], DMA)
            e.dma_start(w2_sb[:, :, :], w_ff2.rearrange("(m p) n -> p m n", p=P)).then_inc(s_w[3], DMA)
            e.wait_ge(s_pool, 10)
            for half in range(2):
                r0 = 64 * half + MROW
                e.dma_start(k_st[r0:r0 + 2, half, :, :].bitcast(F32), hn[0:8, :, :]).then_inc(s_ones, DMA)
            e.wait_ge(s_dve, 6)
            e.dma_start(scratch.rearrange("b r c -> b (r c)"), mod_row[:, :, :].rearrange("b r c -> b (r c)")).then_inc(s_modrow, DMA)
            e.wait_ge(s_dve, 10)
            e.wait_ge(s_pe, 4)
            e.wait_ge(s_act, 4)
            e.dma_start(stage_m, w_mix.rearrange("(k p) n -> p k n", p=P)).then_inc(s_w[2], DMA)
            e.wait_ge(s_modrow, DMA)
            e.wait_ge(s_ones, 2 * DMA)
            batches(e, "sync")
            e.wait_ge(out_s.sem, B * DMA)

        @block.gpsimd
        def _(e):
            e.memset(ident[:, :], 0.0).then_inc(s_pool, 1)
            e.memset(ident_b[:, :], 0.0).then_inc(s_pool, 1)
            e.memset(mask[:, :, :], 0.0).then_inc(s_pool, 1)
            e.memset(mhalf[:, :], -0.5).then_inc(s_pool, 1)
            e.memset(hn[:, :, :], 1.0).then_inc(s_pool, 1)
            e.memset(v_sb[:, :, :], 1.0).then_inc(s_pool, 1)
            e.memset(q_st[:, :, :].bitcast(F32), 0.0).then_inc(s_pool, 1)
            e.memset(k_st[:, 0, :, :].bitcast(F32), 0.0).then_inc(s_pool, 1)
            e.memset(k_st[:, 1, :, :].bitcast(F32), 0.0).then_inc(s_pool, 1)
            e.wait_ge(s_pool, 9)
            e.memset(mask[:, 0, :], NEG).then_inc(s_pool, 1)
            for m in (ident, ident_b):
                e.affine_select(out=m[:, :], in_=m[:, :], compare_op=ALU.not_equal, fill=1.0, base=0,
                                pattern=[[-1, P]], channel_multiplier=1).then_inc(s_pool, 1)
            for i in (1, 3, 5):
                e.affine_select(out=mask[:, i, :], in_=mask[:, i, :], compare_op=ALU.is_ge, fill=NEG, base=0,
                                pattern=[[-1, P]], channel_multiplier=1).then_inc(s_pool, 1)
            for i in (2, 4):
                e.affine_select(out=mask[:, i, :], in_=mask[:, i, :], compare_op=ALU.is_ge, fill=NEG, base=0,
                                pattern=[[1, P]], channel_multiplier=-1).then_inc(s_pool, 1)
            e.wait_ge(s_dve, 11)
            e.wait_ge(s_rows, 2 * DMA)
            e.wait_ge(s_pool, 17)
            batches(e, "gpsimd")

        @block.scalar
        def _(e):
            e.wait_ge(s_ct, DMA)
            e.activation(sct[:, :, :], ct[:, :, :], ACT.Tanh, scale=0.5).then_inc(s_act, 1)
            e.wait_ge(s_col, DMA)
            e.wait_ge(s_w[0], DMA)
            for k in range(KC):
                e.activation(wa_hi[:, k, 0:3 * D], stage_a[:, k, 0:3 * D], ACT.Copy, scale=col[:, c_ln1w + k:c_ln1w + k + 1]).then_inc(s_act, 1)
            e.activation(wa_hi[:, :, 3 * D:4 * D], stage_a[:, :, 3 * D:4 * D], ACT.Copy).then_inc(s_act, 1)
            e.wait_ge(s_w[1], DMA)
            for k in range(KC):
                e.activation(w1_hi[:, k, :], stage_1[:, k, :], ACT.Copy, scale=col[:, c_ln2w + k:c_ln2w + k + 1]).then_inc(s_act, 1)
            e.wait_ge(s_w[2], DMA)
            e.activation(wb_hi[:, :, :], stage_m, ACT.Copy).then_inc(s_act, 1)
            e.wait_ge(s_dve, 14)
            batches(e, "scalar")

        @block.tensor
        def _(e):
            e.wait_ge(s_dve, 1)
            e.wait_ge(s_mod, 3 * DMA)
            for i in range(3):
                for k in range(KC):
                    last = e.matmul(pm[i][0:B, :], sct[:, k, :], wmod_v[i][:, k, :], start=(k == 0), stop=(k == KC - 1))
            last.then_inc(s_pe, 1)
            for j in range(2):
                for m in range(KC):
                    for k in range(KC):
                        src = wmod_v[1][:, k, D + m * P:D + (m + 1) * P] if j == 0 else wmod_v[2][:, k, m * P:(m + 1) * P]
                        u = (2 * j + m) * B
                        last = e.matmul(pc[:, u:u + B], src, sct[:, k, :], start=(k == 0), stop=(k == KC - 1))
            last.then_inc(s_pe, 1)
            e.wait_ge(s_w[0], DMA)
            e.wait_ge(s_col, DMA)
            e.wait_ge(s_w[1], DMA)
            for m in range(6):
                for k in range(KC):
                    e.matmul(pb[:, 64 + m:65 + m], stage_a[:, k, m * P:(m + 1) * P], col[:, c_ln1b + k:c_ln1b + k + 1],
                             start=(k == 0), stop=(k == KC - 1))
            for m in range(MF):
                for k in range(KC):
                    last = e.matmul(pb[:, 72 + m:73 + m], stage_1[:, k, m * P:(m + 1) * P], col[:, c_ln2b + k:c_ln2b + k + 1],
                                    start=(k == 0), stop=(k == KC - 1))
            last.then_inc(s_pe, 1)
            e.wait_ge(s_dve, 9)
            for k in range(KC):
                last = e.matmul(pr[:, 0:D], xa[:, k, 0:P], stage_a[:, k, 3 * D:4 * D], start=(k == 0), stop=(k == KC - 1))
            last.then_inc(s_pe, 1)
            e.wait_ge(s_pool, 17)
            e.wait_ge(s_w[3], DMA)
            e.wait_ge(s_dve, 14)
            e.wait_ge(s_ones, 2 * DMA)
            batches(e, "tensor")

        @block.vector
        def _(e):
            chain = sem("s_chain")
            done = [0]

            def link(ins):
                done[0] += 1
                ins.then_inc(chain, 1)
                e.wait_ge(chain, done[0])

            e.wait_ge(s_act, 1)
            link(e.scalar_tensor_tensor(out=sct[:, :, :], in0=sct[:, :, :], scalar=1.0, in1=ct[:, :, :], op0=ALU.add, op1=ALU.mult))
            e.tensor_scalar(sct[:, :, :], sct[:, :, :], 0.5, None, ALU.mult).then_inc(s_dve, 1)
            e.wait_ge(s_pe, 1)
            e.tensor_scalar(mod_row[:, 0, :], pm[0][0:B, D:2 * D], 1.0, None, ALU.add).then_inc(s_dve, 1)
            e.tensor_copy(mod_row[:, 1, :], pm[0][0:B, 0:D]).then_inc(s_dve, 1)
            for i, (src, factor) in enumerate(((pm[1][0:B, 0:D], 1.0), (pm[2][0:B, D:2 * D], 0.5))):
                link(e.tensor_scalar(mod_x[:, 0, :], src, 0.0, 2.0, ALU.is_ge, ALU.mult))
                link(e.tensor_scalar(mod_x[:, 0, :], mod_x[:, 0, :], -1.0, factor, ALU.add, ALU.mult))
                link(e.tensor_copy(mod_x[:, 1, :], src))
                link(e.scalar_tensor_tensor(out=mod_row[:, 2 + i, :], in0=mod_x[:, 1, :], scalar=-1.0, in1=mod_x[:, 1, :],
                                            op0=ALU.mult, op1=ALU.max))
                e.scalar_tensor_tensor(out=mod_row[:, 2 + i, :], in0=mod_row[:, 2 + i, :], scalar=0.25, in1=mod_x[:, 0, :],
                                       op0=ALU.max, op1=ALU.mult).then_inc(s_dve, 1)
                e.wait_ge(s_dve, 4 + i)
            e.wait_ge(s_pe, 2)
            link(e.tensor_copy(mod_t[:, :, 0:2], pc[:, 0:2 * B].rearrange("p (m b) -> p b m", b=B)))
            e.tensor_scalar(mod_t[:, :, 2:4], pc[:, 2 * B:4 * B].rearrange("p (m b) -> p b m", b=B), 1.0, None, ALU.add).then_inc(s_dve, 1)
            e.wait_ge(s_pe, 3)
            e.tensor_tensor(bias_q[:, :], pb[:, 64:68], col[:, c_bq:c_bq + 4], ALU.add).then_inc(s_dve, 1)
            e.tensor_tensor(bias_1[:, :], pb[:, 72:72 + MF], col[:, c_b1:c_b1 + MF], ALU.add).then_inc(s_dve, 1)
            link(e.tensor_tensor(cv[:, :], pb[:, 68:70], col[:, c_bv:c_bv + KC], ALU.add))
            e.tensor_copy(xa[:, 0:KC, 0:P], cv[:, :].rearrange("p (k o) -> p k o", o=1).broadcast_to([P, KC, P])).then_inc(s_dve, 1)
            e.wait_ge(s_act, 4)
            for k in range(KC):
                link(e.scalar_tensor_tensor(out=wa_lo[:, k, 0:3 * D], in0=stage_a[:, k, 0:3 * D], scalar=col[:, c_ln1w + k:c_ln1w + k + 1],
                                            in1=wa_hi[:, k, 0:3 * D].bitcast(F32), op0=ALU.mult, op1=ALU.subtract))
            e.tensor_tensor(wa_lo[:, :, 3 * D:4 * D], stage_a[:, :, 3 * D:4 * D], wa_hi[:, :, 3 * D:4 * D].bitcast(F32), ALU.subtract).then_inc(s_dve, 1)
            e.wait_ge(s_rows, 2 * DMA)
            e.wait_ge(s_pe, 4)
            e.tensor_tensor(row_o[:, :], pr[:, 0:D], row_o[:, :], ALU.add).then_inc(s_dve, 1)
            e.wait_ge(s_act, 6)
            for k in range(KC):
                e.scalar_tensor_tensor(out=w1_lo[:, k, :], in0=stage_1[:, k, :], scalar=col[:, c_ln2w + k:c_ln2w + k + 1],
                                       in1=w1_hi[:, k, :].bitcast(F32), op0=ALU.mult, op1=ALU.subtract).then_inc(s_dve, 1)
            e.wait_ge(s_act, 7)
            e.tensor_tensor(wb_lo[:, :, :], stage_m, wb_hi[:, :, :].bitcast(F32), ALU.subtract).then_inc(s_dve, 1)
            e.wait_ge(s_dve, 14)
            e.wait_ge(s_pe, 4)
            e.wait_ge(s_pool, 17)
            e.wait_ge(s_ones, 2 * DMA)
            batches(e, "vector")


def kernel(**inputs):
    import concourse.bacc as bacc
    import numpy as np
    from concourse.bass_utils import run_bass_kernel_spmd

    a = {k: np.asarray(v) for k, v in inputs.items()}
    x = a["L0_attn_x"]
    D, H = x.shape[-1], 16
    order = np.arange(D).reshape(2, H // 2, D // H).transpose(0, 2, 1).reshape(-1)
    halves = lambda v: np.ascontiguousarray(v.reshape(-1, 128).T)
    arrays = {
        "x": x,
        "w_attn": np.concatenate([a["L0_attn_Wq"][:, order], a["L0_attn_Wk"][:, order], a["L0_attn_Wv"], a["L0_attn_Wo"]], axis=1),
        "w_ff1": a["L0_attn_W1"],
        "w_ff2": a["L0_attn_W2"],
        "w_mix": np.concatenate([a["L0_ffn_W_r"].T, a["L0_ffn_W_k"].T, a["L0_ffn_W_v"].T], axis=1),
        "w_mod": a["L0_wmod"],
        "c_t": a["L0_c"].T,
        "cols": np.concatenate([halves(v) for v in (
            a["L0_attn_ln1_w"], a["L0_attn_ln1_b"], a["L0_attn_ln2_w"], a["L0_attn_ln2_b"],
            a["L0_attn_bq"][order], a["L0_attn_bk"][order], a["L0_attn_bv"], a["L0_attn_b1"],
            a["L0_ffn_mu_r"], a["L0_ffn_mu_k"])], axis=1),
        "bo": a["L0_attn_bo"],
        "b2": a["L0_attn_b2"],
    }
    arrays = {k: np.ascontiguousarray(v) for k, v in arrays.items()}
    nc = bacc.Bacc("TRN2", target_bir_lowering=False, num_devices=1)
    args = [nc.dram_tensor(k, v.shape, F32, kind="ExternalInput").ap() for k, v in arrays.items()]
    out = nc.dram_tensor("out", x.shape, F32, kind="ExternalOutput").ap()
    adaln_block(nc, *args, out)
    r = run_bass_kernel_spmd(nc, [arrays], core_ids=[0])
    return r.results[0]["out"]
```

```python
from contextlib import ExitStack

import concourse.bass as bass
from concourse import mybir

F32 = mybir.dt.float32
F32R = mybir.dt.float32r
BF16 = mybir.dt.bfloat16
F16 = mybir.dt.float16
ALU = mybir.AluOpType
ACT = mybir.ActivationFunctionType
AX = mybir.AxisListType

P = 128
NEG = -3.0e38
EPS = 1e-5
COST = {"vector": 620, "scalar": 490, "gpsimd": 1200, "sync": 60}
LATENCY, LATENCY_DMA = 120, 2200
DMA = 16


class Signal:

    def __init__(self, sem, unit=1):
        self.sem, self.unit, self.per = sem, unit, 0


class Ring:

    def __init__(self, banks, entry=None):
        self.banks, self.entry, self.uses = banks, entry, []

    def take(self):
        use = {"bank": self.banks[len(self.uses) % len(self.banks)], "n": len(self.uses), "free": None}
        self.uses.append(use)
        return use

    def before(self, use):
        k = len(self.banks)
        if use["n"] >= k:
            return (*self.uses[use["n"] - k]["free"], 0)
        if self.entry is not None:
            return self.entry[use["n"]]()
        assert len(self.uses) % k == 0
        return (*self.uses[len(self.uses) - k + use["n"]]["free"], 1)


    def last(self, k, back=0):
        return (*[u for u in self.uses if u["n"] % len(self.banks) == k][-1]["free"], back)


def wait(eng, signal, n, b):
    per, unit = signal.per, signal.unit
    if isinstance(b, int):
        if b >= 0 and b * per + n > 0:
            eng.wait_ge(signal.sem, (b * per + n) * unit)
    else:
        eng.wait_ge(signal.sem, b * (per * unit) + n * unit)


class Plan:

    def __init__(self):
        self.steps = []

    def do(self, engine, emit, waits=(), signal=None, cost=0, gate=None, after=None):
        n = 0
        if signal is not None:
            signal.per += 1
            n = signal.per

        def run(eng, b):
            for s, count, back in resolved(waits):
                wait(eng, s, count, b - back if back else b)
            if gate is not None and not isinstance(b, int):
                eng.sem_inc(gate, 1)
            last = emit(eng, b)
            if signal is not None:
                last.then_inc(signal.sem, signal.unit)

        self.steps.append((engine, run, cost or COST[engine], waits, signal, n, after))
        return n


def resolved(waits):
    for w in waits:
        w = w() if callable(w) else w
        s, count, back = w if len(w) == 3 else (*w, 0)
        yield s, (s.per if count is None else count), back


def ordered(*parts):
    made = {}
    for steps, offset in parts:
        for step in steps:
            if step[4] is not None:
                made[id(step[4]), offset] = []
    queues, total, done = [], [], []
    for steps, offset in parts:
        q = {}
        for step in steps:
            q.setdefault(step[0], []).append(step)
        queues.append({e: [0, steps_e] for e, steps_e in q.items()})
        total.append(sum(s[2] for s in steps))
        done.append(0)
    free, order, left = {}, [], sum(len(steps) for steps, _ in parts)
    while left:
        best = None
        for p, (steps, offset) in enumerate(parts):
            for engine, (at, queue) in queues[p].items():
                if at == len(queue):
                    continue
                step = queue[at]
                ready = 0
                for s, count, back in resolved(step[3]):
                    ends = made.get((id(s), offset - back))
                    if ends is None:
                        continue
                    if len(ends) < count:
                        ready = None
                        break
                    ready = max(ready, ends[count - 1] + (LATENCY_DMA if s.unit == DMA else LATENCY))
                if step[6] is not None:
                    other, back = step[6]
                    ends = made.get((id(other), offset - back))
                    if ends is not None and len(ends) < other.per:
                        ready = None
                if ready is None:
                    continue
                key = (max(ready, free.get(engine, 0)), done[p] / total[p], p)
                if best is None or key < best[0]:
                    best = key, p, engine, step, offset
        key, p, engine, step, offset = best
        end = key[0] + step[2]
        free[engine] = end
        queues[p][engine][0] += 1
        done[p] += step[2]
        if step[4] is not None:
            made[id(step[4]), offset].append(end)
        order.append((engine, step[1], offset))
        left -= 1
    return order


def adaln_block(nc, x, w_attn, w_ff1, w_ff2, w_mix, w_mod, c_t, cols, bo, b2, out):
    B, L, D = x.shape
    NT = L // P
    KC = D // P
    FF = w_ff1.shape[1]
    MF = FF // P
    H = 16
    HD = D // H
    HS = H // 2
    VW = 3 * HD + 1
    SCALE = float(HD) ** -0.5
    PW = 2 * L - P
    MROW = 3 * HD

    ctx = ExitStack()
    with ctx:
        def sb(name, shape, dt=F32):
            return ctx.enter_context(nc.sbuf_tensor(name, shape, dt))

        def sem(name):
            return ctx.enter_context(nc.semaphore(name))

        def sig(name, unit=1):
            return Signal(sem(name), unit)

        scratch = nc.dram_tensor("mod_rows", (B, 4, D), F32, kind="Internal").ap()

        wa_hi, wa_lo = sb("wa_hi", [P, KC, 4 * D], F32R), sb("wa_lo", [P, KC, 4 * D], F32R)
        w1_hi, w1_lo = sb("w1_hi", [P, KC, FF], F32R), sb("w1_lo", [P, KC, FF], F32R)
        wb_hi, wb_lo = sb("wb_hi", [P, KC, 3 * D], F32R), sb("wb_lo", [P, KC, 3 * D], F32R)
        w2_sb = sb("w2_sb", [P, MF, D])
        ident = sb("ident", [P, P])
        ident_b = sb("ident_b", [P, P], BF16)
        mask = sb("mask", [P, 6, P], BF16)
        mhalf = sb("mhalf", [P, NT])
        col = sb("col", [P, cols.shape[1]])
        bias_q = sb("bias_q", [P, 4])
        bias_1 = sb("bias_1", [P, MF])
        cv = sb("cv", [P, KC])
        ct = sb("ct", [P, KC, B])
        sct = sb("sct", [P, KC, B])
        mod_t = sb("mod_t", [P, B, 4])
        mod_c = sb("mod_c", [P, 4])
        row_o = sb("row_o", [P, D])
        row_2 = sb("row_2", [P, D])
        xa = sb("xa", [P, NT, D])
        mod_a = sb("mod_a", [P, 2, D])
        h = sb("h", [P, NT, D])
        hr = sb("hr", [P, NT, D])
        hn = sb("hn", [P, NT, D])
        cx = sb("cx", [P, NT, D])
        st_a, mv_a = sb("st_a", [P, NT, 6]), sb("mv_a", [P, NT, 2])
        ve_a, rs_a = sb("ve_a", [P, NT]), sb("rs_a", [P, NT])
        at_hi, at_lo = sb("at_hi", [P, KC, L], F32R), sb("at_lo", [P, KC, L], F32R)
        qk_hi, qk_lo = sb("qk_hi", [P, KC, L], F32R), sb("qk_lo", [P, KC, L], F32R)
        q_st = sb("q_st", [P, HS, L], F32R)
        k_st = sb("k_st", [P, 2, HS, L], F32R)
        v_sb = sb("v_sb", [P, NT * H, VW], BF16)
        nmax = sb("nmax", [P, NT, H])
        nm_hl = sb("nm_hl", [P, NT, 2, H], F32R)
        m_t = sb("m_t", [2 * H, L], F32R)
        NP = 3
        p32 = [sb(f"p32_{i}", [P, 2 * L]) for i in range(NP)]
        p_hi = [sb(f"p_hi{i}", [P, PW], F16) for i in range(NP)]
        p_lo = [sb(f"p_lo{i}", [P, PW], F16) for i in range(NP)]
        rsum = sb("rsum", [P, 2, 2 * NT])
        csum = sb("csum", [P, 2, 2 * NT, HD])
        x1 = sb("x1", [P, NT, D])
        x2 = sb("x2", [P, NT, D])
        mod_b = sb("mod_b", [P, 2, D])
        st_b, mv_b = sb("st_b", [P, NT, 6]), sb("mv_b", [P, NT, 2])
        ve_b, rs_b = sb("ve_b", [P, NT]), sb("rs_b", [P, NT])
        bt_hi, bt_lo = sb("bt_hi", [P, KC, L], F32R), sb("bt_lo", [P, KC, L], F32R)
        kt_hi, kt_lo = sb("kt_hi", [P, KC, L], F32R), sb("kt_lo", [P, KC, L], F32R)
        g = sb("g", [P, MF * L + KC])
        hid = g[:, 0:MF * L].rearrange("p (m n) -> p m n", m=MF)
        xrk = g[:, 0:KC * L].rearrange("p (k n) -> p k n", k=KC)
        dif = g[:, 2 * L:4 * L].rearrange("p (k n) -> p k n", k=KC)
        tr = g[:, 4 * L:6 * L].rearrange("p (t n) -> p t n", t=NT)
        n2 = tr
        h3 = g[:, 6 * L:8 * L + KC].rearrange("p (k n) -> p k n", k=KC)

        psum = [ctx.enter_context(nc.psum_tensor(f"bank{i}", [P, 512], F32)) for i in range(8)]
        ring_s = Ring(psum[0:4], [lambda: ring_w.last(0, 1), lambda: ring_f.last(0),
                                  lambda: ring_t.last(0, 1), lambda: ring_t.last(1, 1)])
        ring_w = Ring(psum[0:1], [lambda: ring_s.last(0)])
        ring_f = Ring(psum[1:2], [lambda: ring_s.last(1, 1)])
        ring_t = Ring(psum[2:4], [lambda: ring_s.last(2), lambda: ring_s.last(3)])
        ring_c = Ring(psum[4:6])
        ring_b = Ring(psum[6:8])

        c_ln1w, c_ln1b, c_ln2w, c_ln2b, c_bq, c_bv, c_b1, c_mur, c_muk = 0, 2, 4, 6, 8, 12, 14, 22, 24

        x_t = x.rearrange("b (t p) c -> b p t c", p=P)
        out_t = out.rearrange("b (t p) c -> b p t c", p=P)

        s_pool, s_dve = sem("s_pool"), sem("s_dve")

        tick_v, tick_p = sem("tick_v"), sem("tick_p")

        A0, A1, A2 = Plan(), Plan(), Plan()
        B1, B2 = Plan(), Plan()
        x_in, moda_in = sig("x_in", DMA), sig("moda_in", DMA)
        st0, mv0, ve0, rs0 = sig("st0"), sig("mv0"), sig("ve0"), sig("rs0")
        hpre, hfull = sig("hpre"), sig("hfull")
        st1, mv1, ve1, rs1, hn_s = sig("st1"), sig("mv1"), sig("ve1"), sig("rs1"), sig("hn")
        h_row = sig("h_row")
        tr1, at1_hi, at1_lo = sig("tr1"), sig("at1_hi"), sig("at1_lo")
        qk_mm, qk_h, qk_l = sig("qk_mm"), sig("qk_h"), sig("qk_l")
        stack = [sig(f"stack{m}", DMA) for m in range(4)]
        zero_in, max_in = sig("zero_in", DMA), sig("max_in", DMA)
        v_mm, v1_s, vr_s, v2_s, v3_s = sig("v_mm"), sig("v1"), sig("vr"), sig("v2"), sig("v3")
        s_mm, s_max = sig("s_mm"), sig("s_max")
        nm_hi_s, nm_lo_s, mt_tr, mt_s = sig("nm_hi"), sig("nm_lo"), sig("mt_tr"), sig("mt")
        st_mm, exp_s, sel_s, ph_s = sig("st_mm"), sig("exp"), sig("sel"), sig("p_hi")
        pl_v, pl_g = sig("pl_v"), sig("pl_g")
        av_mm, rcp_s, cs_s, ctx_s = sig("av_mm"), sig("rcp"), sig("csum"), sig("ctx")
        ctr, at2_hi, at2_lo = sig("ctr"), sig("at2_hi"), sig("at2_lo")
        wo_mm, x1_s = sig("wo_mm"), sig("x1")
        x_in_b, modb_in = sig("x_in_b", DMA), sig("modb_in", DMA)
        st2, mv2, ve2, rs2, n2_s = sig("st2"), sig("mv2"), sig("ve2"), sig("rs2"), sig("n2")
        x1_row = sig("x1_row")
        tr2, bt1_hi, bt1_lo = sig("tr2"), sig("bt1_hi"), sig("bt1_lo")
        f1_mm, gelu_s, f2_mm, y_s, yg_s, x2_s = sig("f1_mm"), sig("gelu"), sig("f2_mm"), sig("y"), sig("yg"), sig("x2")
        st3, mv3, ve3, rs3, n3_s = sig("st3"), sig("mv3"), sig("ve3"), sig("rs3"), sig("n3")
        modc_s, zcol = sig("modc"), sig("zcol")
        tr3, h3_s, dif_s = sig("tr3"), sig("h3"), sig("dif")
        xr_s, xr_h, xr_l = sig("xr"), sig("xr_h"), sig("xr_l")
        xk_s, xk_h, xk_l = sig("xk"), sig("xk_h"), sig("xk_l")
        r_mm, r_s, k_mm, relu_s, ksq_s, ka_h, ka_l = (sig(n) for n in ("r_mm", "r", "k_mm", "relu", "ksq", "ka_h", "ka_l"))
        vb_mm, o1_s, o2_s, o3_s, out_s = sig("vb_mm"), sig("o1"), sig("o2"), sig("o3"), sig("out_s", DMA)

        def norm_stats(plan, src, st, mv, ve, rs, s_st, s_mv, s_ve, s_rs, ready, free):
            for t in range(NT):
                plan.do("vector", lambda e, b, t=t: e.bn_stats(st[:, t, :], src[:, t, :]),
                        ready(t) + [free], s_st, 340)
            for t in range(NT):
                plan.do("vector", lambda e, b, t=t: e.bn_aggr(mv[:, t, :], st[:, t, :]),
                        [lambda t=t: (s_st, t + 1)] + [free], s_mv, 80, gate=tick_v)
            plan.do("gpsimd", lambda e, b: e.tensor_scalar(ve[:, :], mv[:, :, 1], 1.0, EPS, ALU.mult, ALU.add),
                    [(s_mv, None)], s_ve, 170, gate=tick_p)
            plan.do("gpsimd", lambda e, b: e.tensor_tensor(rs[:, :], ve[:, :], mhalf[:, :], ALU.pow),
                    [(s_ve, None)], s_rs, 950)

        def transposes(plan, ring, src, k, waits, signal):
            use = ring.take()

            def emit(e, b):
                for t in range(NT):
                    last = e.transpose(use["bank"][:, t * P:(t + 1) * P], src[:, t, k * P:(k + 1) * P], ident[:, :])
                return last
            n = plan.do("tensor", emit, waits + [lambda: ring.before(use)], signal, 4 * 60)
            return use, n

        def three(plan, dst, a_hi, a_lo, b_hi, b_lo, waits, signal, cost):
            for k in range(KC):
                def emit(e, b, k=k):
                    e.matmul(dst, a_hi(k), b_hi(k), start=(k == 0), stop=False)
                    e.matmul(dst, a_hi(k), b_lo(k), start=False, stop=False)
                    return e.matmul(dst, a_lo(k), b_hi(k), start=False, stop=(k == KC - 1))
                plan.do("tensor", emit, waits if k == 0 else [], signal if k == KC - 1 else None, 3 * cost)

        def token_rows(plan, ring, a_hi, a_lo, w_hi, w_lo, c0, waits, signal):
            for t2 in range(NT // 2):
                use = ring.take()
                for t in (2 * t2, 2 * t2 + 1):
                    three(plan, use["bank"][:, (t % 2) * D:(t % 2) * D + D],
                          lambda k, t=t: a_hi[:, k, t * P:(t + 1) * P], lambda k, t=t: a_lo[:, k, t * P:(t + 1) * P],
                          lambda k: w_hi[:, k, c0:c0 + D], lambda k: w_lo[:, k, c0:c0 + D],
                          waits + [lambda use=use: ring.before(use)] if t % 2 == 0 else [],
                          signal if t % 2 else None, 109)
                yield t2, use

        A0.do("sync", lambda e, b: e.dma_start(xa[:, :, :], x_t[b] if isinstance(b, int) else x_t[bass.ds(b, 1)].rearrange("o p t c -> (o p) t c")),
              [(hpre, None, 1)], x_in)
        A0.do("sync", lambda e, b: e.dma_start(mod_a[:, :, :], mod_bcast(b, 0)), [(hfull, None, 1)], moda_in)

        def mod_bcast(b, r):
            s = scratch[b if isinstance(b, int) else bass.ds(b, 1), r:r + 2, :]
            if isinstance(b, int):
                s = s.rearrange("(o r) c -> o r c", o=1)
            return s.broadcast_to([P, 2, D])

        norm_stats(A0, xa, st_a, mv_a, ve_a, rs_a, st0, mv0, ve0, rs0, lambda t: [(x_in, 1)], (hn_s, None, 1))
        for t in range(NT):
            A0.do("vector", lambda e, b, t=t: e.scalar_tensor_tensor(
                out=h[:, t, :], in0=xa[:, t, :], scalar=mv_a[:, t, 0:1], in1=mod_a[:, 0, :],
                op0=ALU.subtract, op1=ALU.mult), [(mv0, NT), (moda_in, 1), (h_row, None, 1)], hpre, 340)
        for t in range(NT):
            A0.do("vector", lambda e, b, t=t: e.scalar_tensor_tensor(
                out=h[:, t, :], in0=h[:, t, :], scalar=rs_a[:, t:t + 1], in1=mod_a[:, 1, :],
                op0=ALU.mult, op1=ALU.add), [(rs0, 1), (hpre, t + 1)], hfull, 340)
        norm_stats(A0, h, st_a, mv_a, ve_a, rs_a, st1, mv1, ve1, rs1, lambda t: [(hfull, t + 1), (mv0, t + 1)], (hfull, NT))
        for t in range(NT):
            A0.do("vector", lambda e, b, t=t: e.tensor_scalar(
                hn[:, t, :], h[:, t, :], mv_a[:, t, 0:1], rs_a[:, t:t + 1], ALU.subtract, ALU.mult),
                [(rs1, 1), (tr1, None, 1)], hn_s, 330)
        A1.do("gpsimd", lambda e, b: e.tensor_tensor(
            hr[:, :, :], h[:, :, :], row_o[:, :].rearrange("p (o c) -> p o c", o=1).broadcast_to([P, NT, D]), ALU.add),
            [(hfull, None), (x1_s, None, 1)], h_row, 2300)
        for k in range(KC):
            use, n = transposes(A0, ring_f, hn, k, [(hn_s, NT)], tr1)
            A0.do("scalar", lambda e, b, k=k, use=use: e.activation(at_hi[:, k, :], use["bank"][:, :], ACT.Copy),
                  [(tr1, n), (v_mm, None, 1)], at1_hi)
            m = A0.do("vector", lambda e, b, k=k, use=use: e.tensor_tensor(
                at_lo[:, k, :], use["bank"][:, :], at_hi[:, k, :].bitcast(F32), ALU.subtract),
                [(at1_hi, k + 1), (v_mm, None, 1)], at1_lo)
            use["free"] = (at1_lo, m)
        A1.do("sync", lambda e, b: e.dma_start(q_st[MROW:MROW + 2, :, :].bitcast(F32), k_st[64:64 + 2, 0, :, :].bitcast(F32)),
              [(st_mm, None, 1)], zero_in)
        A1.do("sync", lambda e, b: e.dma_start(q_st[64 + MROW:64 + MROW + 2, :, :].bitcast(F32), k_st[64:64 + 2, 0, :, :].bitcast(F32)),
              [], zero_in)
        for m in range(4):
            is_k, half = m % 2, m // 2
            c0 = is_k * D + half * P
            use = ring_s.take()
            slot = m % 2
            three(A1, use["bank"][:, :], lambda k, c0=c0: wa_hi[:, k, c0:c0 + P], lambda k, c0=c0: wa_lo[:, k, c0:c0 + P],
                  lambda k: at_hi[:, k, :], lambda k: at_lo[:, k, :],
                  [(at1_lo, KC), lambda use=use: ring_s.before(use)], qk_mm, 216)
            bias = bias_q[:, 2 * is_k + half:2 * is_k + half + 1]
            free = (stack[m - 2], 3) if m >= 2 else (wo_mm, None, 1)
            A1.do("scalar", lambda e, b, use=use, slot=slot, bias=bias: e.activation(
                qk_hi[:, slot, :], use["bank"][:, :], ACT.Identity, bias=bias), [(qk_mm, m + 1), free], qk_h)
            n = A1.do("vector", lambda e, b, use=use, slot=slot, bias=bias: e.scalar_tensor_tensor(
                out=qk_lo[:, slot, :], in0=use["bank"][:, :], scalar=bias, in1=qk_hi[:, slot, :].bitcast(F32),
                op0=ALU.add, op1=ALU.subtract), [(qk_h, m + 1), free], qk_l)
            use["free"] = (qk_l, n)
            src = [qk_hi, qk_hi, qk_lo] if is_k else [qk_hi, qk_lo, qk_hi]
            for j in range(3):
                r0 = 64 * half + HD * j
                dst = k_st[r0:r0 + HD, half, :, :] if is_k else q_st[r0:r0 + HD, :, :]
                A1.do("sync", lambda e, b, dst=dst, s=src[j], slot=slot: e.dma_start(dst.bitcast(F32), s[:, slot, :].bitcast(F32)),
                      [(qk_l, m + 1), (st_mm, None, 1)] if j == 0 else [], stack[m])
        for t2, use in token_rows(A1, ring_s, at_hi, at_lo, wa_hi, wa_lo, 2 * D, [], v_mm):
            rows = slice(2 * t2 * H, (2 * t2 + 2) * H)
            bank = use["bank"][:, :].rearrange("p (u d) -> p u d", d=HD)
            rest = cx[:, 2 * t2:2 * t2 + 2, :].rearrange("p t (u d) -> p (t u) d", d=HD)
            A1.do("scalar", lambda e, b, rows=rows, bank=bank: e.activation(v_sb[:, rows, 0:HD], bank, ACT.Copy),
                  [(v_mm, t2 + 1), (av_mm, None, 1)], v1_s)
            n = A1.do("vector", lambda e, b, rows=rows, bank=bank, rest=rest: e.tensor_tensor(
                rest, bank, v_sb[:, rows, 0:HD], ALU.subtract), [(v1_s, t2 + 1), (ctr, None, 1)], vr_s)
            use["free"] = (vr_s, n)
            A1.do("scalar", lambda e, b, rows=rows, rest=rest: e.activation(v_sb[:, rows, HD:2 * HD], rest, ACT.Copy),
                  [(vr_s, t2 + 1)], v2_s)
            A1.do("vector", lambda e, b, rows=rows, rest=rest: e.tensor_tensor(
                v_sb[:, rows, 2 * HD:3 * HD], rest, v_sb[:, rows, HD:2 * HD], ALU.subtract),
                [(v2_s, t2 + 1)], v3_s)
        for hd in range(H):
            half, j = hd // HS, hd % HS
            for q2 in range(NT // 2):
                use = ring_s.take()

                def emit(e, b, half=half, j=j, q2=q2, use=use):
                    e.matmul(use["bank"][:, :], ident_b[:, :], mask[:, 2 * q2:2 * q2 + 4, :].rearrange("p a c -> p (a c)"),
                             start=True, stop=False)
                    for qt in (2 * q2, 2 * q2 + 1):
                        lo = max(qt - 1, 0) * P
                        c1 = (qt % 2 + 1) * 2 * P
                        last = e.matmul(use["bank"][:, c1 - ((qt + 1) * P - lo):c1], q_st[:, j, qt * P:(qt + 1) * P],
                                        k_st[:, half, j, lo:(qt + 1) * P], start=False, stop=(qt % 2 == 1))
                    return last
                w = [(stack[m], 3) for m in range(4)] + [(zero_in, 2)] if hd == 0 and q2 == 0 else []
                A1.do("tensor", emit, w + [lambda use=use: ring_s.before(use)], s_mm, 434)
                n = A1.do("vector", lambda e, b, hd=hd, q2=q2, use=use: e.tensor_reduce(
                    nmax[:, 2 * q2:2 * q2 + 2, hd], use["bank"][:, :].rearrange("p (t k) -> p t k", t=2),
                    AX.X, ALU.max, negate=True), [(s_mm, 2 * hd + q2 + 1), (nm_lo_s, None, 1)], s_max)
                use["free"] = (s_max, n)
        A1.do("vector", lambda e, b: e.tensor_copy(nm_hl[:, :, 0, :], nmax[:, :, :]), [(s_max, None), (mt_tr, None, 1)], nm_hi_s, 110)
        A1.do("vector", lambda e, b: e.tensor_tensor(nm_hl[:, :, 1, :], nmax[:, :, :], nm_hl[:, :, 0, :].bitcast(F32), ALU.subtract),
              [(nm_hi_s, 1)], nm_lo_s, 150)
        use_m = ring_s.take()

        def emit(e, b):
            for t in range(NT):
                last = e.transpose(use_m["bank"][0:2 * H, t * P:(t + 1) * P],
                                   nm_hl[:, t, :, :].rearrange("p a c -> p (a c)").bitcast(F32), ident[:, :])
            return last
        A1.do("tensor", emit, [(nm_lo_s, 1), lambda: ring_s.before(use_m)], mt_tr, 240)
        n = A1.do("vector", lambda e, b: e.tensor_copy(m_t[:, :], use_m["bank"][0:2 * H, :]),
                  [(mt_tr, 1), (max_in, None, 1)], mt_s)
        use_m["free"] = (mt_s, n)
        for half in range(2):
            for part in range(2):
                r0, s0 = 64 * half + MROW + part, part * H + half * HS
                A1.do("sync", lambda e, b, r0=r0, s0=s0: e.dma_start(q_st[r0:r0 + 1, :, :].bitcast(F32), m_t[s0:s0 + HS, :].bitcast(F32)),
                      [(mt_s, None), (s_mm, None)] if half == part == 0 else [], max_in)

        def scores_t(hd):
            half, j, slot = hd // HS, hd % HS, hd % NP
            for k2 in range(NT // 2):
                use = ring_t.take()

                def emit(e, b, use=use, k2=k2):
                    for kt in (2 * k2, 2 * k2 + 1):
                        n = min(2 * P, L - kt * P)
                        c0 = (kt % 2) * 2 * P
                        last = e.matmul(use["bank"][:, c0:c0 + n], k_st[:, half, j, kt * P:(kt + 1) * P],
                                        q_st[:, j, kt * P:kt * P + n], start=True, stop=True)
                    return last
                A2.do("tensor", emit, ([(max_in, 4)] if hd == 0 and k2 == 0 else []) + [lambda use=use: ring_t.before(use)],
                      st_mm, 218 if k2 == 0 else 165)
                c0, n = k2 * 4 * P, min(4 * P, PW - k2 * 4 * P)
                m = A2.do("scalar", lambda e, b, use=use, c0=c0, n=n: e.activation(
                    p32[slot][:, c0:c0 + n], use["bank"][:, 0:n], ACT.Exp, scale=SCALE),
                    [(st_mm, 2 * hd + k2 + 1), low_of(hd - NP)], exp_s, 480 if k2 == 0 else 370, after=(gelu_s, 1))
                use["free"] = (exp_s, m)
            A2.do("gpsimd", lambda e, b: e.affine_select(
                out=blocks(p32[slot], 0, NT), in_=blocks(p32[slot], 0, NT), compare_op=ALU.is_ge, fill=0.0, base=0,
                pattern=[[0, NT], [1, P]], channel_multiplier=-1), [(exp_s, 2 * hd + 2)], sel_s, 580, gate=tick_p)
            A2.do("gpsimd", lambda e, b: e.affine_select(
                out=blocks(p32[slot], 1, NT - 1), in_=blocks(p32[slot], 1, NT - 1), compare_op=ALU.is_ge, fill=0.0, base=0,
                pattern=[[0, NT - 1], [-1, P]], channel_multiplier=1), [], sel_s, 460)

        def split_p(hd):
            slot = hd % NP
            free = (av_mm, hd - NP + 1) if hd >= NP else av_before(hd)
            A2.do("scalar", lambda e, b: e.activation(p_hi[slot][:, :], p32[slot][:, 0:PW], ACT.Copy),
                  [(sel_s, 2 * hd + 2), free], ph_s, 800)
            A2.do("gpsimd" if on_pool(hd) else "vector", lambda e, b: e.tensor_tensor(
                p_lo[slot][:, :], p32[slot][:, 0:PW], p_hi[slot][:, :], ALU.subtract),
                [(ph_s, hd + 1), free], pl_g if on_pool(hd) else pl_v, 1980 if on_pool(hd) else 1000)

        def blocks(tile, k, n):
            return tile[:, 0:2 * L].rearrange("p (t c) -> p t c", t=NT)[:, 0:n, k * P:(k + 1) * P]

        def on_pool(hd):
            return hd % 2 == 1

        def slot_before(hd):
            return max(i for i in range(H) if i % NP == hd % NP)

        def av_before(hd):
            return (av_mm, slot_before(hd) + 1, 1)

        def low_of(hd):
            back = 0
            if hd < 0:
                hd, back = slot_before(hd + NP), 1
            return (pl_g if on_pool(hd) else pl_v, sum(on_pool(i) == on_pool(hd) for i in range(hd + 1)), back)

        uses_c = {}

        def context(hd):
            slot, pair = hd % NP, hd // 2
            if hd % 2 == 0:
                uses_c[pair] = ring_c.take()
            use = uses_c[pair]

            def emit(e, b):
                for qt in range(NT):
                    u = (hd % 2) * NT + qt
                    dst = use["bank"][:, u * VW:(u + 1) * VW]
                    pieces = [(pt[slot], kt, qt - kt) for pt in (p_hi, p_lo) for kt in range(max(qt - 1, 0), qt + 1)]
                    for i, (pt, kt, k) in enumerate(pieces):
                        c0 = kt * 2 * P + k * P
                        last = e.matmul(dst, pt[:, c0:c0 + P], v_sb[:, kt * H + hd, :],
                                        start=(i == 0), stop=(i == len(pieces) - 1))
                return last
            w = [low_of(hd)] + ([lambda use=use: ring_c.before(use)] if hd % 2 == 0 else [])
            A2.do("tensor", emit, w + ([(v3_s, None)] if hd == 0 else []), av_mm, 14 * 35)
            if hd % 2 == 0:
                return
            s2 = pair % 2
            bank = use["bank"][:, 0:2 * NT * VW].rearrange("p (u w) -> p u w", w=VW)
            A2.do("vector", lambda e, b: e.reciprocal(rsum[:, s2, :], bank[:, :, VW - 1]),
                  [(av_mm, hd + 1), (ctx_s, pair - 1) if pair >= 2 else (ctx_s, H // 2 - 1 + pair, 1)], rcp_s, 80)
            n = A2.do("vector", lambda e, b: e.tensor_reduce(
                csum[:, s2, :, :], bank[:, :, 0:3 * HD].rearrange("p u (s d) -> p u d s", s=3), AX.X, ALU.add),
                [], cs_s, 470)
            use["free"] = (cs_s, n)
            dst = cx[:, :, (hd - 1) * HD:(hd + 1) * HD].rearrange("p t (u d) -> p u t d", u=2)
            A2.do("vector", lambda e, b: e.tensor_tensor(
                dst, csum[:, s2, :, :].rearrange("p (u t) d -> p u t d", u=2),
                rsum[:, s2, :].rearrange("p (u t o) -> p u t o", u=2, o=1).broadcast_to([P, 2, NT, HD]), ALU.mult),
                [(cs_s, pair + 1), (v3_s, None)], ctx_s, 210)

        for hd in range(H + 2):
            if hd < H:
                scores_t(hd)
            if 1 <= hd <= H:
                split_p(hd - 1)
            if hd >= 2:
                context(hd - 2)
        for k in range(KC):
            use, n = transposes(A2, ring_w, cx, k, [(ctx_s, None)], ctr)
            A2.do("scalar", lambda e, b, k=k, use=use: e.activation(qk_hi[:, k, :], use["bank"][:, :], ACT.Copy),
                  [(ctr, n), (stack[3], 3), (stack[2], 3)], at2_hi)
            m = A2.do("vector", lambda e, b, k=k, use=use: e.tensor_tensor(
                qk_lo[:, k, :], use["bank"][:, :], qk_hi[:, k, :].bitcast(F32), ALU.subtract), [(at2_hi, k + 1)], at2_lo)
            use["free"] = (at2_lo, m)
        for t2, use in token_rows(A2, ring_w, qk_hi, qk_lo, wa_hi, wa_lo, 3 * D, [(at2_lo, KC)], wo_mm):
            n = A2.do("vector", lambda e, b, t2=t2, use=use: e.tensor_tensor(
                x1[:, 2 * t2:2 * t2 + 2, :], use["bank"][:, :].rearrange("p (t c) -> p t c", t=2),
                hr[:, 2 * t2:2 * t2 + 2, :], ALU.add), [(wo_mm, t2 + 1), (h_row, 1), (x2_s, None, 1)], x1_s)
            use["free"] = (x1_s, n)

        B1.do("sync", lambda e, b: e.dma_start(mod_b[:, :, :], mod_bcast(b, 2)), [(o2_s, None, 1)], modb_in)
        B1.do("sync", lambda e, b: e.dma_start(x2[:, :, :], x_t[b] if isinstance(b, int) else x_t[bass.ds(b, 1)].rearrange("o p t c -> (o p) t c")),
              [(out_s, None, 1)], x_in_b)
        B1.do("vector", lambda e, b: e.tensor_copy(mod_c[:, :], mod_t[:, b, :] if isinstance(b, int) else mod_t[:, bass.ds(b, 1), :].rearrange("p o f -> p (o f)")),
              [(h3_s, None, 1)], modc_s, 80)
        norm_stats(B1, x1, st_b, mv_b, ve_b, rs_b, st2, mv2, ve2, rs2, lambda t: [(x1_s, None)], (n3_s, None, 1))
        for t in range(NT):
            B1.do("vector", lambda e, b, t=t: e.tensor_scalar(
                n2[:, t, :], x1[:, t, :], mv_b[:, t, 0:1], rs_b[:, t:t + 1], ALU.subtract, ALU.mult),
                [(rs2, 1), (o3_s, None, 1)], n2_s, 330)
        B1.do("gpsimd", lambda e, b: e.tensor_tensor(
            x1[:, :, :], x1[:, :, :], row_2[:, :].rearrange("p (o c) -> p o c", o=1).broadcast_to([P, NT, D]), ALU.add),
            [(n2_s, NT)], x1_row, 2300)
        for k in range(KC):
            use, n = transposes(B1, ring_b, n2, k, [(n2_s, NT)], tr2)
            B1.do("scalar", lambda e, b, k=k, use=use: e.activation(bt_hi[:, k, :], use["bank"][:, :], ACT.Copy),
                  [(tr2, n), (vb_mm, None, 1)], bt1_hi)
            m = B1.do("vector", lambda e, b, k=k, use=use: e.tensor_tensor(
                bt_lo[:, k, :], use["bank"][:, :], bt_hi[:, k, :].bitcast(F32), ALU.subtract),
                [(bt1_hi, k + 1), (vb_mm, None, 1)], bt1_lo)
            use["free"] = (bt1_lo, m)
        for m in range(MF):
            use = ring_b.take()
            three(B1, use["bank"][:, :], lambda k, m=m: w1_hi[:, k, m * P:(m + 1) * P], lambda k, m=m: w1_lo[:, k, m * P:(m + 1) * P],
                  lambda k: bt_hi[:, k, :], lambda k: bt_lo[:, k, :],
                  [(bt1_lo, KC), lambda use=use: ring_b.before(use)], f1_mm, 216)
            n = B1.do("scalar", lambda e, b, m=m, use=use: e.activation(
                hid[:, m, :], use["bank"][:, :], ACT.Gelu_apprx_tanh, bias=bias_1[:, m:m + 1]),
                [(f1_mm, m + 1), (o1_s, None, 1), (ksq_s, None, 1), (xk_l, None, 1)], gelu_s, 570)
            use["free"] = (gelu_s, n)
        for t2 in range(NT // 2):
            use = ring_b.take()

            for t in (2 * t2, 2 * t2 + 1):
                for m0 in range(0, MF, 2):
                    def emit(e, b, t=t, m0=m0, use=use):
                        for m in (m0, m0 + 1):
                            last = e.matmul(use["bank"][:, (t % 2) * D:(t % 2) * D + D], hid[:, m, t * P:(t + 1) * P],
                                            w2_sb[:, m, :], start=(m == 0), stop=(m == MF - 1))
                        return last
                    B2.do("tensor", emit, [(gelu_s, MF), lambda use=use: ring_b.before(use)] if t % 2 == m0 == 0 else [],
                          f2_mm if t % 2 and m0 == MF - 2 else None, 864)
            ts = slice(2 * t2, 2 * t2 + 2)
            n = B2.do("vector", lambda e, b, ts=ts, use=use: e.tensor_tensor(
                x1[:, ts, :], use["bank"][:, :].rearrange("p (t c) -> p t c", t=2), x1[:, ts, :], ALU.add),
                [(f2_mm, t2 + 1), (x1_row, 1)], y_s)
            use["free"] = (y_s, n)
            B2.do("gpsimd", lambda e, b, ts=ts: e.tensor_tensor(
                x1[:, ts, :], x1[:, ts, :], mod_b[:, 0:1, :].broadcast_to([P, 2, D]), ALU.mult),
                [(y_s, t2 + 1), (modb_in, 1)], yg_s)
            B2.do("vector", lambda e, b, ts=ts: e.tensor_tensor(
                x2[:, ts, :], x2[:, ts, :], x1[:, ts, :], ALU.add), [(yg_s, t2 + 1), (x_in_b, 1)], x2_s)
        norm_stats(B2, x2, st_b, mv_b, ve_b, rs_b, st3, mv3, ve3, rs3, lambda t: [(x2_s, t // 2 + 1), (mv2, t + 1)], (n2_s, NT))
        for t in range(NT):
            B2.do("vector", lambda e, b, t=t: e.tensor_scalar(
                n2[:, t, :], x2[:, t, :], mv_b[:, t, 0:1], rs_b[:, t:t + 1], ALU.subtract, ALU.mult),
                [(rs3, 1), (f2_mm, None)], n3_s, 330)
        B2.do("vector", lambda e, b: e.memset(h3[:, :, 0:1], 0.0), [(f2_mm, None)], zcol, 60)
        for k in range(KC):
            use, n = transposes(B2, ring_b, n2, k, [(n3_s, NT)], tr3)
            m = B2.do("scalar", lambda e, b, k=k, use=use: e.activation(
                h3[:, k, 1:L + 1], use["bank"][:, :], ACT.Identity, bias=mod_c[:, k:k + 1], scale=mod_c[:, KC + k:KC + k + 1]),
                [(tr3, n), (modc_s, 1), (f2_mm, None)], h3_s)
            use["free"] = (h3_s, m)
        B2.do("gpsimd", lambda e, b: e.tensor_tensor(dif, h3[:, :, 1:L + 1], h3[:, :, 0:L], ALU.subtract),
              [(h3_s, KC), (zcol, 1), (f2_mm, None)], dif_s, 2300)
        for c_mu, s_x, s_h, s_l, hi, lo, free in ((c_mur, xr_s, xr_h, xr_l, bt_hi, bt_lo, (f1_mm, None)),
                                                  (c_muk, xk_s, xk_h, xk_l, kt_hi, kt_lo, (k_mm, None, 1))):
            for k in range(KC):
                w = [(dif_s, 1)] if s_x is xr_s else [(xr_l, k + 1)]
                B2.do("vector", lambda e, b, k=k, c_mu=c_mu: e.scalar_tensor_tensor(
                    out=xrk[:, k, :], in0=dif[:, k, :], scalar=col[:, c_mu + k:c_mu + k + 1], in1=h3[:, k, 0:L],
                    op0=ALU.mult, op1=ALU.add), w, s_x)
                B2.do("scalar", lambda e, b, k=k, hi=hi: e.activation(hi[:, k, :], xrk[:, k, :], ACT.Copy),
                      [(s_x, k + 1), free], s_h)
                B2.do("vector", lambda e, b, k=k, hi=hi, lo=lo: e.tensor_tensor(
                    lo[:, k, :], xrk[:, k, :], hi[:, k, :].bitcast(F32), ALU.subtract), [(s_h, k + 1), free], s_l)

        for t2, use in token_rows(B2, ring_b, bt_hi, bt_lo, wb_hi, wb_lo, 0, [(xr_l, KC)], r_mm):
            n = B2.do("scalar", lambda e, b, t2=t2, use=use: e.activation(
                tr[:, 2 * t2:2 * t2 + 2, :], use["bank"][:, :].rearrange("p (t c) -> p t c", t=2), ACT.Tanh, scale=0.5),
                [(r_mm, t2 + 1), (f2_mm, None)], r_s)
            use["free"] = (r_s, n)
        for m in range(KC):
            use = ring_b.take()
            three(B2, use["bank"][:, :], lambda k, m=m: wb_hi[:, k, D + m * P:D + (m + 1) * P],
                  lambda k, m=m: wb_lo[:, k, D + m * P:D + (m + 1) * P], lambda k: kt_hi[:, k, :], lambda k: kt_lo[:, k, :],
                  [(xk_l, KC), lambda use=use: ring_b.before(use)], k_mm, 216)
            n = B2.do("scalar", lambda e, b, m=m, use=use: e.activation(xrk[:, m, :], use["bank"][:, :], ACT.Relu),
                      [(k_mm, m + 1), (xk_l, KC)], relu_s)
            use["free"] = (relu_s, n)
            B2.do("scalar", lambda e, b, m=m: e.activation(dif[:, m, :], xrk[:, m, :], ACT.Square),
                  [(relu_s, m + 1), (xk_s, KC)], ksq_s)
            B2.do("scalar", lambda e, b, m=m: e.activation(bt_hi[:, m, :], dif[:, m, :], ACT.Copy),
                  [(ksq_s, m + 1), (r_mm, None)], ka_h)
            B2.do("vector", lambda e, b, m=m: e.tensor_tensor(
                bt_lo[:, m, :], dif[:, m, :], bt_hi[:, m, :].bitcast(F32), ALU.subtract),
                [(ka_h, m + 1), (r_mm, None)], ka_l)
        for t2, use in token_rows(B2, ring_b, bt_hi, bt_lo, wb_hi, wb_lo, 2 * D, [(ka_l, KC)], vb_mm):
            ts = slice(2 * t2, 2 * t2 + 2)
            n = B2.do("vector", lambda e, b, ts=ts, use=use: e.scalar_tensor_tensor(
                out=tr[:, ts, :].rearrange("p t c -> p (t c)"), in0=tr[:, ts, :].rearrange("p t c -> p (t c)"), scalar=1.0,
                in1=use["bank"][:, :], op0=ALU.add, op1=ALU.mult),
                [(vb_mm, t2 + 1), (r_s, t2 + 1)], o1_s)
            use["free"] = (o1_s, n)
            B2.do("gpsimd", lambda e, b, ts=ts: e.tensor_tensor(
                tr[:, ts, :], tr[:, ts, :], mod_b[:, 1:2, :].broadcast_to([P, 2, D]), ALU.mult), [(o1_s, t2 + 1)], o2_s)
            B2.do("vector", lambda e, b, ts=ts: e.tensor_tensor(x2[:, ts, :], x2[:, ts, :], tr[:, ts, :], ALU.add),
                  [(o2_s, t2 + 1), (n3_s, NT)], o3_s)
        B2.do("sync", lambda e, b: e.dma_start(out_t[b] if isinstance(b, int) else out_t[bass.ds(b, 1)].rearrange("o p t c -> (o p) t c"), x2[:, :, :]),
              [(o3_s, None)], out_s)

        def body(next_batch=True, stage_b=True):
            parts = [(A1.steps + A2.steps, 0)]
            if stage_b:
                parts.append((B1.steps + B2.steps, -1))
            if next_batch:
                parts.append((A0.steps, 1))
            return ordered(*parts)

        orders = {"head": ordered((A0.steps, 0)), "first": body(stage_b=False), "each": body(),
                  "last": body(next_batch=False), "tail": ordered((B1.steps + B2.steps, 0))}

        def play(eng, name, order, b):
            for engine, run, offset in order:
                if engine == name:
                    run(eng, b + offset if offset else b)

        def batches(eng, name):
            play(eng, name, orders["head"], 0)
            play(eng, name, orders["first"], 0)
            play(eng, name, orders["each"], 1)
            with eng.Fori(2, B - 1) as i:
                play(eng, name, orders["each"], i)
            play(eng, name, orders["last"], B - 1)
            play(eng, name, orders["tail"], B - 1)

        s_col, s_ct, s_mod, s_rows = sem("s_col"), sem("s_ct"), sem("s_mod"), sem("s_rows")
        s_w = [sem(f"s_w{i}") for i in range(4)]
        s_act, s_pe = sem("s_act"), sem("s_pe")
        s_ones, s_scr, s_modrow = sem("s_ones"), sem("s_scr"), sem("s_modrow")
        mod_row = cx[0:B, :, :]
        mod_x = p32[0][0:B, 0:2 * D].rearrange("b (r c) -> b r c", r=2)
        stage = [g[:, 0:8 * D], g[:, 8 * D:16 * D]]
        stage_a = stage[0].rearrange("p (k n) -> p k n", k=KC)
        stage_1 = stage[1].rearrange("p (k n) -> p k n", k=KC)
        stage_m = stage[0][:, 0:KC * 3 * D].rearrange("p (k n) -> p k n", k=KC)
        wmod = [x1, x2, hr]
        wmod_v = [t[:, :, :].rearrange("p (k a) c -> p k (a c)", k=KC) for t in wmod]
        pm = psum[0:3]
        pc = psum[3]
        pb = psum[5]
        pr = psum[4]

        block = ctx.enter_context(nc.Block())

        @block.sync
        def _(e):
            e.dma_start(col[:, :], cols).then_inc(s_col, DMA)
            e.dma_start(ct[:, :, :], c_t.rearrange("(k p) b -> p k b", p=P)).then_inc(s_ct, DMA)
            for i in range(3):
                e.dma_start(wmod_v[i], w_mod[:, i * 2 * D:(i + 1) * 2 * D].rearrange("(k p) n -> p k n", p=P)).then_inc(s_mod, DMA)
            e.dma_start(stage_a, w_attn.rearrange("(k p) n -> p k n", p=P)).then_inc(s_w[0], DMA)
            e.dma_start(row_o[:, :], bo.rearrange("(o c) -> o c", o=1).broadcast_to([P, D])).then_inc(s_rows, DMA)
            e.dma_start(row_2[:, :], b2.rearrange("(o c) -> o c", o=1).broadcast_to([P, D])).then_inc(s_rows, DMA)
            e.dma_start(stage_1, w_ff1.rearrange("(k p) n -> p k n", p=P)).then_inc(s_w[1], DMA)
            e.dma_start(w2_sb[:, :, :], w_ff2.rearrange("(m p) n -> p m n", p=P)).then_inc(s_w[3], DMA)
            e.wait_ge(s_pool, 10)
            for half in range(2):
                r0 = 64 * half + MROW
                e.dma_start(k_st[r0:r0 + 2, half, :, :].bitcast(F32), hn[0:8, :, :]).then_inc(s_ones, DMA)
            e.wait_ge(s_dve, 6)
            e.dma_start(scratch.rearrange("b r c -> b (r c)"), mod_row[:, :, :].rearrange("b r c -> b (r c)")).then_inc(s_modrow, DMA)
            e.wait_ge(s_dve, 10)
            e.wait_ge(s_pe, 4)
            e.wait_ge(s_act, 4)
            e.dma_start(stage_m, w_mix.rearrange("(k p) n -> p k n", p=P)).then_inc(s_w[2], DMA)
            e.wait_ge(s_modrow, DMA)
            e.wait_ge(s_ones, 2 * DMA)
            batches(e, "sync")
            e.wait_ge(out_s.sem, B * DMA)

        @block.gpsimd
        def _(e):
            e.memset(ident[:, :], 0.0).then_inc(s_pool, 1)
            e.memset(ident_b[:, :], 0.0).then_inc(s_pool, 1)
            e.memset(mask[:, :, :], 0.0).then_inc(s_pool, 1)
            e.memset(mhalf[:, :], -0.5).then_inc(s_pool, 1)
            e.memset(hn[:, :, :], 1.0).then_inc(s_pool, 1)
            e.memset(v_sb[:, :, :], 1.0).then_inc(s_pool, 1)
            e.memset(q_st[:, :, :].bitcast(F32), 0.0).then_inc(s_pool, 1)
            e.memset(k_st[:, 0, :, :].bitcast(F32), 0.0).then_inc(s_pool, 1)
            e.memset(k_st[:, 1, :, :].bitcast(F32), 0.0).then_inc(s_pool, 1)
            e.wait_ge(s_pool, 9)
            e.memset(mask[:, 0, :], NEG).then_inc(s_pool, 1)
            for m in (ident, ident_b):
                e.affine_select(out=m[:, :], in_=m[:, :], compare_op=ALU.not_equal, fill=1.0, base=0,
                                pattern=[[-1, P]], channel_multiplier=1).then_inc(s_pool, 1)
            for i in (1, 3, 5):
                e.affine_select(out=mask[:, i, :], in_=mask[:, i, :], compare_op=ALU.is_ge, fill=NEG, base=0,
                                pattern=[[-1, P]], channel_multiplier=1).then_inc(s_pool, 1)
            for i in (2, 4):
                e.affine_select(out=mask[:, i, :], in_=mask[:, i, :], compare_op=ALU.is_ge, fill=NEG, base=0,
                                pattern=[[1, P]], channel_multiplier=-1).then_inc(s_pool, 1)
            e.wait_ge(s_dve, 11)
            e.wait_ge(s_rows, 2 * DMA)
            e.wait_ge(s_pool, 17)
            batches(e, "gpsimd")

        @block.scalar
        def _(e):
            e.wait_ge(s_ct, DMA)
            e.activation(sct[:, :, :], ct[:, :, :], ACT.Tanh, scale=0.5).then_inc(s_act, 1)
            e.wait_ge(s_col, DMA)
            e.wait_ge(s_w[0], DMA)
            for k in range(KC):
                e.activation(wa_hi[:, k, 0:3 * D], stage_a[:, k, 0:3 * D], ACT.Copy, scale=col[:, c_ln1w + k:c_ln1w + k + 1]).then_inc(s_act, 1)
            e.activation(wa_hi[:, :, 3 * D:4 * D], stage_a[:, :, 3 * D:4 * D], ACT.Copy).then_inc(s_act, 1)
            e.wait_ge(s_w[1], DMA)
            for k in range(KC):
                e.activation(w1_hi[:, k, :], stage_1[:, k, :], ACT.Copy, scale=col[:, c_ln2w + k:c_ln2w + k + 1]).then_inc(s_act, 1)
            e.wait_ge(s_w[2], DMA)
            e.activation(wb_hi[:, :, :], stage_m, ACT.Copy).then_inc(s_act, 1)
            e.wait_ge(s_dve, 14)
            batches(e, "scalar")

        @block.tensor
        def _(e):
            e.wait_ge(s_dve, 1)
            e.wait_ge(s_mod, 3 * DMA)
            for i in range(3):
                for k in range(KC):
                    last = e.matmul(pm[i][0:B, :], sct[:, k, :], wmod_v[i][:, k, :], start=(k == 0), stop=(k == KC - 1))
            last.then_inc(s_pe, 1)
            for j in range(2):
                for m in range(KC):
                    for k in range(KC):
                        src = wmod_v[1][:, k, D + m * P:D + (m + 1) * P] if j == 0 else wmod_v[2][:, k, m * P:(m + 1) * P]
                        u = (2 * j + m) * B
                        last = e.matmul(pc[:, u:u + B], src, sct[:, k, :], start=(k == 0), stop=(k == KC - 1))
            last.then_inc(s_pe, 1)
            e.wait_ge(s_w[0], DMA)
            e.wait_ge(s_col, DMA)
            e.wait_ge(s_w[1], DMA)
            for m in range(6):
                for k in range(KC):
                    e.matmul(pb[:, 64 + m:65 + m], stage_a[:, k, m * P:(m + 1) * P], col[:, c_ln1b + k:c_ln1b + k + 1],
                             start=(k == 0), stop=(k == KC - 1))
            for m in range(MF):
                for k in range(KC):
                    last = e.matmul(pb[:, 72 + m:73 + m], stage_1[:, k, m * P:(m + 1) * P], col[:, c_ln2b + k:c_ln2b + k + 1],
                                    start=(k == 0), stop=(k == KC - 1))
            last.then_inc(s_pe, 1)
            e.wait_ge(s_dve, 9)
            for k in range(KC):
                last = e.matmul(pr[:, 0:D], xa[:, k, 0:P], stage_a[:, k, 3 * D:4 * D], start=(k == 0), stop=(k == KC - 1))
            last.then_inc(s_pe, 1)
            e.wait_ge(s_pool, 17)
            e.wait_ge(s_w[3], DMA)
            e.wait_ge(s_dve, 14)
            e.wait_ge(s_ones, 2 * DMA)
            batches(e, "tensor")

        @block.vector
        def _(e):
            chain = sem("s_chain")
            done = [0]

            def link(ins):
                done[0] += 1
                ins.then_inc(chain, 1)
                e.wait_ge(chain, done[0])

            e.wait_ge(s_act, 1)
            link(e.scalar_tensor_tensor(out=sct[:, :, :], in0=sct[:, :, :], scalar=1.0, in1=ct[:, :, :], op0=ALU.add, op1=ALU.mult))
            e.tensor_scalar(sct[:, :, :], sct[:, :, :], 0.5, None, ALU.mult).then_inc(s_dve, 1)
            e.wait_ge(s_pe, 1)
            e.tensor_scalar(mod_row[:, 0, :], pm[0][0:B, D:2 * D], 1.0, None, ALU.add).then_inc(s_dve, 1)
            e.tensor_copy(mod_row[:, 1, :], pm[0][0:B, 0:D]).then_inc(s_dve, 1)
            for i, (src, factor) in enumerate(((pm[1][0:B, 0:D], 1.0), (pm[2][0:B, D:2 * D], 0.5))):
                link(e.tensor_scalar(mod_x[:, 0, :], src, 0.0, 2.0, ALU.is_ge, ALU.mult))
                link(e.tensor_scalar(mod_x[:, 0, :], mod_x[:, 0, :], -1.0, factor, ALU.add, ALU.mult))
                link(e.tensor_copy(mod_x[:, 1, :], src))
                link(e.scalar_tensor_tensor(out=mod_row[:, 2 + i, :], in0=mod_x[:, 1, :], scalar=-1.0, in1=mod_x[:, 1, :],
                                            op0=ALU.mult, op1=ALU.max))
                e.scalar_tensor_tensor(out=mod_row[:, 2 + i, :], in0=mod_row[:, 2 + i, :], scalar=0.25, in1=mod_x[:, 0, :],
                                       op0=ALU.max, op1=ALU.mult).then_inc(s_dve, 1)
                e.wait_ge(s_dve, 4 + i)
            e.wait_ge(s_pe, 2)
            link(e.tensor_copy(mod_t[:, :, 0:2], pc[:, 0:2 * B].rearrange("p (m b) -> p b m", b=B)))
            e.tensor_scalar(mod_t[:, :, 2:4], pc[:, 2 * B:4 * B].rearrange("p (m b) -> p b m", b=B), 1.0, None, ALU.add).then_inc(s_dve, 1)
            e.wait_ge(s_pe, 3)
            e.tensor_tensor(bias_q[:, :], pb[:, 64:68], col[:, c_bq:c_bq + 4], ALU.add).then_inc(s_dve, 1)
            e.tensor_tensor(bias_1[:, :], pb[:, 72:72 + MF], col[:, c_b1:c_b1 + MF], ALU.add).then_inc(s_dve, 1)
            link(e.tensor_tensor(cv[:, :], pb[:, 68:70], col[:, c_bv:c_bv + KC], ALU.add))
            e.tensor_copy(xa[:, 0:KC, 0:P], cv[:, :].rearrange("p (k o) -> p k o", o=1).broadcast_to([P, KC, P])).then_inc(s_dve, 1)
            e.wait_ge(s_act, 4)
            for k in range(KC):
                link(e.scalar_tensor_tensor(out=wa_lo[:, k, 0:3 * D], in0=stage_a[:, k, 0:3 * D], scalar=col[:, c_ln1w + k:c_ln1w + k + 1],
                                            in1=wa_hi[:, k, 0:3 * D].bitcast(F32), op0=ALU.mult, op1=ALU.subtract))
            e.tensor_tensor(wa_lo[:, :, 3 * D:4 * D], stage_a[:, :, 3 * D:4 * D], wa_hi[:, :, 3 * D:4 * D].bitcast(F32), ALU.subtract).then_inc(s_dve, 1)
            e.wait_ge(s_rows, 2 * DMA)
            e.wait_ge(s_pe, 4)
            e.tensor_tensor(row_o[:, :], pr[:, 0:D], row_o[:, :], ALU.add).then_inc(s_dve, 1)
            e.wait_ge(s_act, 6)
            for k in range(KC):
                e.scalar_tensor_tensor(out=w1_lo[:, k, :], in0=stage_1[:, k, :], scalar=col[:, c_ln2w + k:c_ln2w + k + 1],
                                       in1=w1_hi[:, k, :].bitcast(F32), op0=ALU.mult, op1=ALU.subtract).then_inc(s_dve, 1)
            e.wait_ge(s_act, 7)
            e.tensor_tensor(wb_lo[:, :, :], stage_m, wb_hi[:, :, :].bitcast(F32), ALU.subtract).then_inc(s_dve, 1)
            e.wait_ge(s_dve, 14)
            e.wait_ge(s_pe, 4)
            e.wait_ge(s_pool, 17)
            e.wait_ge(s_ones, 2 * DMA)
            batches(e, "vector")


def kernel(**inputs):
    import concourse.bacc as bacc
    import numpy as np
    from concourse.bass_utils import run_bass_kernel_spmd

    a = {k: np.asarray(v) for k, v in inputs.items()}
    x = a["L0_attn_x"]
    D, H = x.shape[-1], 16
    order = np.arange(D).reshape(2, H // 2, D // H).transpose(0, 2, 1).reshape(-1)
    halves = lambda v: np.ascontiguousarray(v.reshape(-1, 128).T)
    arrays = {
        "x": x,
        "w_attn": np.concatenate([a["L0_attn_Wq"][:, order], a["L0_attn_Wk"][:, order], a["L0_attn_Wv"], a["L0_attn_Wo"]], axis=1),
        "w_ff1": a["L0_attn_W1"],
        "w_ff2": a["L0_attn_W2"],
        "w_mix": np.concatenate([a["L0_ffn_W_r"].T, a["L0_ffn_W_k"].T, a["L0_ffn_W_v"].T], axis=1),
        "w_mod": a["L0_wmod"],
        "c_t": a["L0_c"].T,
        "cols": np.concatenate([halves(v) for v in (
            a["L0_attn_ln1_w"], a["L0_attn_ln1_b"], a["L0_attn_ln2_w"], a["L0_attn_ln2_b"],
            a["L0_attn_bq"][order], a["L0_attn_bk"][order], a["L0_attn_bv"], a["L0_attn_b1"],
            a["L0_ffn_mu_r"], a["L0_ffn_mu_k"])], axis=1),
        "bo": a["L0_attn_bo"],
        "b2": a["L0_attn_b2"],
    }
    arrays = {k: np.ascontiguousarray(v) for k, v in arrays.items()}
    nc = bacc.Bacc("TRN2", target_bir_lowering=False, num_devices=1, dynamic_dma_scratch_size=1024)
    args = [nc.dram_tensor(k, v.shape, F32, kind="ExternalInput").ap() for k, v in arrays.items()]
    out = nc.dram_tensor("out", x.shape, F32, kind="ExternalOutput").ap()
    adaln_block(nc, *args, out)
    r = run_bass_kernel_spmd(nc, [arrays], core_ids=[0])
    return r.results[0]["out"]
```

```python
from contextlib import ExitStack

import concourse.bass as bass
from concourse import mybir

F32 = mybir.dt.float32
F32R = mybir.dt.float32r
BF16 = mybir.dt.bfloat16
F16 = mybir.dt.float16
ALU = mybir.AluOpType
ACT = mybir.ActivationFunctionType
AX = mybir.AxisListType

P = 128
NEG = -3.0e38
EPS = 1e-5
COST = {"vector": 610, "scalar": 510, "gpsimd": 1230, "sync": 600}
TABLE = 1300
LATENCY, LATENCY_DMA = 180, 2400
DMA = 16
LOW_ON_POOL = (0, 1, 2, 3, 5, 6, 7, 8, 11, 13, 14, 15)
FIRST = {
    "A2": {"tensor": -0.3, "vector": 0.0, "scalar": 0.0, "gpsimd": 0.0},
    "A1": {"tensor": 0.7, "vector": -0.2, "scalar": 1.0, "gpsimd": -0.1},
    "A0": {"tensor": -0.8, "vector": -0.9, "scalar": -0.8, "gpsimd": -0.8},
    "B2": {"tensor": -0.5, "vector": 0.2, "scalar": 0.3, "gpsimd": 0.4},
    "B1": {"tensor": -0.5, "vector": -0.5, "scalar": -0.5, "gpsimd": -0.7},
    "W": {"tensor": -1, "vector": -1, "scalar": -1},
}
PATIENCE = {"gpsimd": 400}


class Signal:

    def __init__(self, sem, unit=1):
        self.sem, self.unit, self.per = sem, unit, 0


class Ring:

    def __init__(self, banks):
        self.banks, self.uses = banks, []

    def take(self):
        use = {"bank": self.banks[len(self.uses) % len(self.banks)], "n": len(self.uses), "free": None}
        self.uses.append(use)
        return use

    def before(self, use):
        k = len(self.banks)
        if use["n"] >= k:
            return (*self.uses[use["n"] - k]["free"], 0)
        assert len(self.uses) % k == 0
        return (*self.uses[len(self.uses) - k + use["n"]]["free"], 1)


def wait(eng, signal, n, b):
    per, unit = signal.per, signal.unit
    n = per if n is None else n
    if isinstance(b, int):
        if b >= 0 and b * per + n > 0:
            eng.wait_ge(signal.sem, (b * per + n) * unit)
    else:
        eng.wait_ge(signal.sem, b * (per * unit) + n * unit)


class Plan:

    def __init__(self):
        self.steps = []

    def do(self, engine, emit, waits=(), signal=None, cost=0, gate=None, table=None):
        n = 0
        if signal is not None:
            signal.per += 1
            n = signal.per

        def run(eng, b):
            for s, count, back in resolved(waits):
                wait(eng, s, count, b - back if back else b)
            if gate is not None and not isinstance(b, int):
                eng.sem_inc(gate, 1)
            last = emit(eng, b)
            if signal is not None:
                last.then_inc(signal.sem, signal.unit)

        self.steps.append((engine, run, cost or COST[engine], waits, signal, n, table))
        return n


def resolved(waits):
    for w in waits:
        w = w() if callable(w) else w
        s, count, back = w if len(w) == 3 else (*w, 0)
        yield s, (s.per if count is None else count), back


class Order:

    def __init__(self):
        self.free = {}
        self.ends = {}
        self.table = "exp"

    def ready(self, step, b):
        at = 0
        for s, count, back in resolved(step[3]):
            ends = self.ends.get((id(s), b - back), {})
            for n in range(count, 0, -1):
                if n in ends:
                    if ends[n] is None:
                        return None
                    at = max(at, ends[n] + (LATENCY_DMA if s.unit == DMA else LATENCY))
                    break
        return at

    def place(self, step, b, start):
        self.free[step[0]] = start + step[2]
        if step[4] is not None:
            self.ends[id(step[4]), b][step[5]] = start + step[2]
        self.table = step[6] or self.table

    def start(self, step, at):
        return max(at, self.free.get(step[0], 0)) + (TABLE if step[6] not in (None, self.table) else 0)

    def turn(self, parts, b):
        queues = []
        for part, _ in parts:
            q = {}
            for steps, offset in part:
                for step in steps:
                    q.setdefault(step[0], []).append((step, offset))
                    if step[4] is not None:
                        self.ends.setdefault((id(step[4]), b + offset), {})[step[5]] = None
            queues.append(q)
        total = [sum(step[2] for steps, _ in part for step in steps) for part, _ in parts]
        done = [0] * len(parts)
        order, left, held = [], sum(len(q) for queue in queues for q in queue.values()), False
        while left:
            first = {}
            for p, queue in enumerate(queues):
                for engine, q in queue.items():
                    if not q or (held and q[0][0][6] == "exp"):
                        continue
                    at = self.ready(q[0][0], b + q[0][1])
                    if at is not None:
                        first.setdefault(engine, []).append(
                            (self.start(q[0][0], at), done[p] / total[p] - FIRST[parts[p][1]].get(engine, 0), p))
            engine = min(first, key=lambda e: min(first[e]))
            soon = min(first[engine])[0] + PATIENCE.get(engine, 0)
            _, start, p = min((rank, start, p) for start, rank, p in first[engine] if start <= soon)
            step, offset = queues[p][engine].pop(0)
            self.place(step, b + offset, start)
            done[p] += step[2]
            if step[6] is not None:
                held = step[6] == "gelu" and step[5] < step[4].per
            order.append((step, offset))
            left -= 1
        return order

    def again(self, order, b):
        for step, offset in order:
            if step[4] is not None:
                self.ends.setdefault((id(step[4]), b + offset), {})[step[5]] = None
        for step, offset in order:
            self.place(step, b + offset, self.start(step, self.ready(step, b + offset)))


def adaln_block(nc, x, w_attn, w_ff1, w_ff2, w_mix, w_mod, c_t, cols, bo, b2, out):
    B, L, D = x.shape
    NT = L // P
    KC = D // P
    FF = w_ff1.shape[1]
    MF = FF // P
    H = 16
    HD = D // H
    HS = H // 2
    HQ = HS // 2
    VW = 3 * HD + 1
    SCALE = float(HD) ** -0.5
    PW = 2 * L - P
    MROW = 3 * HD

    ctx = ExitStack()
    with ctx:
        def sb(name, shape, dt=F32):
            return ctx.enter_context(nc.sbuf_tensor(name, shape, dt))

        def sem(name):
            return ctx.enter_context(nc.semaphore(name))

        def sig(name, unit=1):
            return Signal(sem(name), unit)

        scratch = nc.dram_tensor("mod_rows", (B, 4, D), F32, kind="Internal").ap()

        wa_hi, wa_lo = sb("wa_hi", [P, KC, 4 * D], F32R), sb("wa_lo", [P, KC, 4 * D], F32R)
        w1_hi, w1_lo = sb("w1_hi", [P, KC, FF], F32R), sb("w1_lo", [P, KC, FF], F32R)
        wb_hi, wb_lo = sb("wb_hi", [P, KC, 3 * D], F32R), sb("wb_lo", [P, KC, 3 * D], F32R)
        w2_sb = sb("w2_sb", [P, MF, D])
        ident = sb("ident", [P, P])
        ident_b = sb("ident_b", [P, P], BF16)
        mask = sb("mask", [P, 6, P], BF16)
        mhalf = sb("mhalf", [P, NT])
        col = sb("col", [P, cols.shape[1]])
        bias_q = sb("bias_q", [P, 4])
        bias_1 = sb("bias_1", [P, MF])
        cv = sb("cv", [P, KC])
        ct = sb("ct", [P, KC, B])
        sct = sb("sct", [P, KC, B])
        mod_t = sb("mod_t", [P, B, 4])
        mod_c = sb("mod_c", [P, 4])
        row_o = sb("row_o", [P, D])
        row_2 = sb("row_2", [P, D])
        xa = sb("xa", [P, NT, D])
        mod_a = sb("mod_a", [P, 2, D])
        h = sb("h", [P, NT, D])
        hr = sb("hr", [P, NT, D])
        cx = sb("cx", [P, NT, D])
        st_a, mv_a = sb("st_a", [P, NT, 6]), sb("mv_a", [P, NT, 2])
        ve_a, rs_a = sb("ve_a", [P, NT]), sb("rs_a", [P, NT])
        at_hi, at_lo = sb("at_hi", [P, KC, L], F32R), sb("at_lo", [P, KC, L], F32R)
        qk_hi, qk_lo = sb("qk_hi", [P, 2, L], F32R), sb("qk_lo", [P, 2, L], F32R)
        ct_hi, ct_lo = sb("ct_hi", [P, KC, L], F32R), sb("ct_lo", [P, KC, L], F32R)
        q_st = sb("q_st", [P, 2, HQ, L], F32R)
        k_st = sb("k_st", [P, 2, 2, HQ, L], F32R)
        v_sb = sb("v_sb", [P, NT * H, VW], BF16)
        nmax = sb("nmax", [P, NT, H])
        nm_hl = sb("nm_hl", [P, NT, 2, 2, HQ], F32R)
        m_t = sb("m_t", [2 * HS, L], F32R)
        NP = 3
        p32 = [sb(f"p32_{i}", [P, 2 * L]) for i in range(NP)]
        p_hi = [sb(f"p_hi{i}", [P, PW], F16) for i in range(NP)]
        p_lo = [sb(f"p_lo{i}", [P, PW], F16) for i in range(NP)]
        rsum = sb("rsum", [P, 2, 2 * NT])
        csum = sb("csum", [P, 2, 2 * NT, HD])
        x1 = sb("x1", [P, NT, D])
        x2 = sb("x2", [P, NT, D])
        mod_b = sb("mod_b", [P, 2, D])
        st_b, mv_b = sb("st_b", [P, NT, 6]), sb("mv_b", [P, NT, 2])
        ve_b, rs_b = sb("ve_b", [P, NT]), sb("rs_b", [P, NT])
        bt_hi, bt_lo = sb("bt_hi", [P, KC, L], F32R), sb("bt_lo", [P, KC, L], F32R)
        kt_hi, kt_lo = sb("kt_hi", [P, KC, L], F32R), sb("kt_lo", [P, KC, L], F32R)
        g = sb("g", [P, 2, MF * 2 * P + KC])
        hid = g[:, :, 0:MF * 2 * P].rearrange("p t (m n) -> p t m n", m=MF)
        norm = g[:, :, 0:2 * D].rearrange("p h (t c) -> p h t c", c=D)
        dif = g[:, :, 0:2 * D].rearrange("p h (k n) -> p h k n", k=KC)
        xrk = g[:, :, 2 * D:4 * D].rearrange("p h (k n) -> p h k n", k=KC)
        tr = g[:, :, 4 * D:6 * D]
        h3 = g[:, :, 6 * D:8 * D + KC].rearrange("p h (k n) -> p h k n", k=KC)
        psum = [ctx.enter_context(nc.psum_tensor(f"bank{i}", [P, 512], F32)) for i in range(8)]
        ring_s = Ring(psum[0:2])
        ring_t = Ring(psum[2:4])
        ring_c = Ring(psum[4:6])
        ring_b = Ring(psum[6:8])

        c_ln1w, c_ln1b, c_ln2w, c_ln2b, c_bq, c_bv, c_b1, c_mur, c_muk = 0, 2, 4, 6, 8, 12, 14, 22, 24

        x_t = x.rearrange("b (t p) c -> b p t c", p=P)
        out_t = out.rearrange("b (t p) c -> b p t c", p=P)

        s_pool, s_dve = sem("s_pool"), sem("s_dve")

        tick_v, tick_p = sem("tick_v"), sem("tick_p")

        XA, A0 = Plan(), Plan()
        A1 = [Plan(), Plan()]
        A2 = [Plan(), Plan()]
        B1, B2 = Plan(), Plan()
        x_in, moda_in = sig("x_in", DMA), sig("moda_in", DMA)
        st0, mv0, ve0, rs0 = sig("st0"), sig("mv0"), sig("ve0"), sig("rs0")
        hpre, hfull = sig("hpre"), sig("hfull")
        st1, mv1, ve1, rs1, hn_s = sig("st1"), sig("mv1"), sig("ve1"), sig("rs1"), sig("hn")
        h_row = sig("h_row")
        tr1, at1_hi, at1_lo = sig("tr1"), sig("at1_hi"), sig("at1_lo")
        qk_mm, qk_h, qk_l = sig("qk_mm"), sig("qk_h"), sig("qk_l")
        stack = [sig(f"stack{m}", DMA) for m in range(4)]
        zero_in, max_in = sig("zero_in", DMA), sig("max_in", DMA)
        v_mm, v0_s, v1_s, vr_s, v2_s, v3_s = sig("v_mm"), sig("v0"), sig("v1"), sig("vr"), sig("v2"), sig("v3")
        s_mm, s_max = sig("s_mm"), sig("s_max")
        nm_hi_s, nm_lo_s, mt_tr, mt_s = sig("nm_hi"), sig("nm_lo"), sig("mt_tr"), sig("mt")
        st_mm, exp_s, sel_s, ph_s = sig("st_mm"), sig("exp"), sig("sel"), sig("p_hi")
        pl_v, pl_g = sig("pl_v"), sig("pl_g")
        av_mm, rcp_s, cs_s, ctx_s = sig("av_mm"), sig("rcp"), sig("csum"), sig("ctx")
        ctr, at2_hi, at2_lo = sig("ctr"), sig("at2_hi"), sig("at2_lo")
        wo_mm, x1_s = sig("wo_mm"), sig("x1")
        x_in_b, modb_in = sig("x_in_b", DMA), sig("modb_in", DMA)
        st2, mv2, ve2, rs2, n2_s = sig("st2"), sig("mv2"), sig("ve2"), sig("rs2"), sig("n2")
        x1_row = sig("x1_row")
        tr2, bt1_hi, bt1_lo = sig("tr2"), sig("bt1_hi"), sig("bt1_lo")
        f1_mm, gelu_s, f2_mm, y_s, yg_s, x2_s = sig("f1_mm"), sig("gelu"), sig("f2_mm"), sig("y"), sig("yg"), sig("x2")
        st3, mv3, ve3, rs3, n3_s = sig("st3"), sig("mv3"), sig("ve3"), sig("rs3"), sig("n3")
        modc_s, zcol = sig("modc"), sig("zcol")
        tr3, h3_s, dif_s = sig("tr3"), sig("h3"), sig("dif")
        xr_s, xr_h, xr_l = sig("xr"), sig("xr_h"), sig("xr_l")
        xk_s, xk_h, xk_l = sig("xk"), sig("xk_h"), sig("xk_l")
        r_mm, r_s, k_mm, relu_s, ksq_s, ka_h, ka_l = (sig(n) for n in ("r_mm", "r", "k_mm", "relu", "ksq", "ka_h", "ka_l"))
        vb_mm, o1_s, o2_s, o3_s, out_s = sig("vb_mm"), sig("o1"), sig("o2"), sig("o3"), sig("out_s", DMA)

        def norm_stats(plan, src, tiles, st, mv, ve, rs, s_st, s_mv, s_ve, s_rs, ready, free):
            ts = slice(tiles[0], tiles[-1] + 1)
            for t in tiles:
                plan.do("vector", lambda e, b, t=t: e.bn_stats(st[:, t, :], src[:, t, :]),
                        ready(t) + [free], s_st, 340)
            for t in tiles:
                last = plan.do("vector", lambda e, b, t=t: e.bn_aggr(mv[:, t, :], st[:, t, :]),
                               [(s_st, t + 1), free], s_mv, 80, gate=tick_v)
            n = plan.do("gpsimd", lambda e, b: e.tensor_scalar(ve[:, ts], mv[:, ts, 1], 1.0, EPS, ALU.mult, ALU.add),
                        [(s_mv, last)], s_ve, 170, gate=tick_p)
            plan.do("gpsimd", lambda e, b: e.tensor_tensor(rs[:, ts], ve[:, ts], mhalf[:, ts], ALU.pow),
                    [(s_ve, n)], s_rs, 950)

        def transposes(plan, ring, src, blocks, waits, signal):
            use = ring.take()

            def emit(e, b):
                for i, (t, k) in enumerate(blocks):
                    last = e.transpose(use["bank"][:, i * P:(i + 1) * P], src(t)[:, k * P:(k + 1) * P], ident[:, :])
                return last
            n = plan.do("tensor", emit, waits + [lambda: ring.before(use)], signal, 430)
            return use, n

        def three(plan, dst, a_hi, a_lo, b_hi, b_lo, waits, signal, cost):
            for k in range(KC):
                def emit(e, b, k=k):
                    e.matmul(dst, a_hi(k), b_hi(k), start=(k == 0), stop=False)
                    e.matmul(dst, a_hi(k), b_lo(k), start=False, stop=False)
                    return e.matmul(dst, a_lo(k), b_hi(k), start=False, stop=(k == KC - 1))
                plan.do("tensor", emit, waits if k == 0 else [], signal if k == KC - 1 else None, 3 * cost)

        def token_rows(plan, ring, t2, a_hi, a_lo, w_hi, w_lo, c0, waits, signal):
            use = ring.take()
            for i in range(2):
                t = 2 * t2 + i
                three(plan, use["bank"][:, i * D:(i + 1) * D],
                      lambda k, t=t: a_hi[:, k, t * P:(t + 1) * P], lambda k, t=t: a_lo[:, k, t * P:(t + 1) * P],
                      lambda k: w_hi[:, k, c0:c0 + D], lambda k: w_lo[:, k, c0:c0 + D],
                      waits + [lambda: ring.before(use)] if i == 0 else [], signal if i else None, 109)
            return use

        def split(plan, hi, lo, src, waits, s_hi, s_lo):
            n = plan.do("scalar", lambda e, b: e.activation(hi, src, ACT.Copy), waits, s_hi)
            return plan.do("vector", lambda e, b: e.tensor_tensor(lo, src, hi.bitcast(F32), ALU.subtract),
                           [(s_hi, n)] + waits[1:], s_lo)

        def mod_bcast(b, r):
            s = scratch[b if isinstance(b, int) else bass.ds(b, 1), r:r + 2, :]
            if isinstance(b, int):
                s = s.rearrange("(o r) c -> o r c", o=1)
            return s.broadcast_to([P, 2, D])

        def of_batch(t, b):
            return t[b] if isinstance(b, int) else t[bass.ds(b, 1)].rearrange("o p t c -> (o p) t c")

        def before(signal, n, k=1):
            return lambda: (signal, n - k) if n > k else (signal, signal.per + n - k, 1)

        XA.do("sync", lambda e, b: e.dma_start(xa[:, :, :], of_batch(x_t, b)), [(v3_s, None, 1)], x_in)
        A0.do("sync", lambda e, b: e.dma_start(mod_a[:, :, :], mod_bcast(b, 0)), [(hfull, None, 1)], moda_in)
        tiles = list(range(NT))
        norm_stats(A0, xa, tiles, st_a, mv_a, ve_a, rs_a, st0, mv0, ve0, rs0, lambda t: [(x_in, 1)], (hn_s, None, 1))
        for t in tiles:
            A0.do("vector", lambda e, b, t=t: e.scalar_tensor_tensor(
                out=h[:, t, :], in0=xa[:, t, :], scalar=mv_a[:, t, 0:1], in1=mod_a[:, 0, :],
                op0=ALU.subtract, op1=ALU.mult), [(mv0, NT), (moda_in, 1), (h_row, None, 1)], hpre, 340)
        for t in tiles:
            A0.do("vector", lambda e, b, t=t: e.scalar_tensor_tensor(
                out=h[:, t, :], in0=h[:, t, :], scalar=rs_a[:, t:t + 1], in1=mod_a[:, 1, :],
                op0=ALU.mult, op1=ALU.add), [(rs0, 1), (hpre, t + 1)], hfull, 340)
        norm_stats(A0, h, tiles, st_a, mv_a, ve_a, rs_a, st1, mv1, ve1, rs1, lambda t: [(hfull, t + 1), (mv0, t + 1)], (hfull, NT))
        for t in tiles:
            A0.do("vector", lambda e, b, t=t: e.tensor_scalar(
                xa[:, t, :], h[:, t, :], mv_a[:, t, 0:1], rs_a[:, t:t + 1], ALU.subtract, ALU.mult), [(rs1, 1)], hn_s, 330)
        for k in range(KC):
            use, n = transposes(A0, ring_s, lambda t: xa[:, t, :], [(t, k) for t in tiles], [(hn_s, NT)], tr1)
            use["free"] = (at1_lo, split(A0, at_hi[:, k, :], at_lo[:, k, :], use["bank"][:, :],
                                         [(tr1, n), (v_mm, None, 1), (qk_mm, None, 1)], at1_hi, at1_lo))

        def queries_keys(plan, half):
            for a in range(2):
                r0 = 64 * a + MROW
                plan.do("sync", lambda e, b, r0=r0: e.dma_start(
                    q_st[r0:r0 + 2, half, :, :].bitcast(F32), k_st[64:66, half, 0, :, :].bitcast(F32)),
                    [(st_mm, (half + 1) * HS * 2, 1)] if a == 0 else [], zero_in)
            for is_k in range(2):
                m, c0 = 2 * half + is_k, is_k * D + half * P
                use = ring_s.take()
                three(plan, use["bank"][:, :], lambda k, c0=c0: wa_hi[:, k, c0:c0 + P], lambda k, c0=c0: wa_lo[:, k, c0:c0 + P],
                      lambda k: at_hi[:, k, :], lambda k: at_lo[:, k, :],
                      [(at1_lo, KC), lambda use=use: ring_s.before(use)], qk_mm, 216)
                bias = bias_q[:, m:m + 1]
                free = (stack[m - 2], 6) if half else (stack[m + 2], 6, 1)
                plan.do("scalar", lambda e, b, use=use, is_k=is_k, bias=bias: e.activation(
                    qk_hi[:, is_k, :], use["bank"][:, :], ACT.Identity, bias=bias), [(qk_mm, m + 1), free], qk_h)
                n = plan.do("vector", lambda e, b, use=use, is_k=is_k, bias=bias: e.scalar_tensor_tensor(
                    out=qk_lo[:, is_k, :], in0=use["bank"][:, :], scalar=bias, in1=qk_hi[:, is_k, :].bitcast(F32),
                    op0=ALU.add, op1=ALU.subtract), [(qk_h, m + 1), free], qk_l)
                use["free"] = (qk_l, n)
                for i, src in enumerate([qk_hi, qk_hi, qk_lo] if is_k else [qk_hi, qk_lo, qk_hi]):
                    for a in range(2):
                        r0 = 64 * a + HD * i
                        dst = k_st[r0:r0 + HD, half, a, :, :] if is_k else q_st[r0:r0 + HD, half, :, :]
                        plan.do("sync", lambda e, b, dst=dst, src=src, a=a, is_k=is_k: e.dma_start(
                            dst.bitcast(F32), src[64 * a:64 * a + 64, is_k, :].bitcast(F32)),
                            [(qk_l, m + 1), (st_mm, (half + 1) * HS * 2, 1)] if i == a == 0 else [], stack[m])

        def values(plan):
            for t2 in range(NT // 2):
                use = token_rows(plan, ring_s, t2, at_hi, at_lo, wa_hi, wa_lo, 2 * D, [], v_mm)
                use["free"] = (v0_s, plan.do("scalar", lambda e, b, t2=t2, use=use: e.activation(
                    xa[:, 2 * t2:2 * t2 + 2, :].rearrange("p t c -> p (t c)"), use["bank"][:, :], ACT.Copy), [(v_mm, t2 + 1)], v0_s))

        def split_values(plan, half):
            heads = slice(half * HS, (half + 1) * HS)
            rest = xa[:, :, :].rearrange("p t (u d) -> p t u d", d=HD)[:, :, heads, :]
            parts = v_sb[:, :, :].rearrange("p (t u) w -> p t u w", t=NT)[:, :, heads, :]
            free = (av_mm, (half + 1) * HS, 1)
            plan.do("scalar", lambda e, b: e.activation(parts[:, :, :, 0:HD], rest, ACT.Copy), [(v0_s, None), free], v1_s)
            plan.do("vector", lambda e, b: e.tensor_tensor(rest, rest, parts[:, :, :, 0:HD], ALU.subtract), [(v1_s, half + 1)], vr_s)
            plan.do("scalar", lambda e, b: e.activation(parts[:, :, :, HD:2 * HD], rest, ACT.Copy), [(vr_s, half + 1)], v2_s)
            plan.do("vector", lambda e, b: e.tensor_tensor(
                parts[:, :, :, 2 * HD:3 * HD], rest, parts[:, :, :, HD:2 * HD], ALU.subtract), [(v2_s, half + 1)], v3_s)

        def place(hd):
            return hd // HS, hd % HS // HQ, hd % HQ

        def row_maxima(plan, half):
            for hd in range(half * HS, (half + 1) * HS):
                _, a, j = place(hd)
                for q2 in range(NT // 2):
                    use = ring_s.take()

                    def emit(e, b, a=a, j=j, q2=q2, use=use):
                        e.matmul(use["bank"][:, :], ident_b[:, :], mask[:, 2 * q2:2 * q2 + 4, :].rearrange("p a c -> p (a c)"),
                                 start=True, stop=False)
                        for qt in (2 * q2, 2 * q2 + 1):
                            lo = max(qt - 1, 0) * P
                            c1 = (qt % 2 + 1) * 2 * P
                            last = e.matmul(use["bank"][:, c1 - ((qt + 1) * P - lo):c1], q_st[:, half, j, qt * P:(qt + 1) * P],
                                            k_st[:, half, a, j, lo:(qt + 1) * P], start=False, stop=(qt % 2 == 1))
                        return last
                    w = [(stack[2 * half], 6), (stack[2 * half + 1], 6), (zero_in, 2 * half + 2)] if hd % HS == 0 and q2 == 0 else []
                    n = plan.do("tensor", emit, w + [lambda use=use: ring_s.before(use)], s_mm, 434)
                    n = plan.do("vector", lambda e, b, hd=hd, q2=q2, use=use: e.tensor_reduce(
                        nmax[:, 2 * q2:2 * q2 + 2, hd], use["bank"][:, :].rearrange("p (t k) -> p t k", t=2),
                        AX.X, ALU.max, negate=True), [(s_mm, n), (nm_lo_s, half + 1, 1)], s_max)
                    use["free"] = (s_max, n)
            all_max = (half + 1) * HS * NT // 2
            mx = nmax[:, :, half * HS:(half + 1) * HS].rearrange("p t (a j) -> p t a j", a=2)
            plan.do("vector", lambda e, b: e.tensor_copy(nm_hl[:, :, :, 0, :], mx),
                    [(s_max, all_max), before(mt_tr, half + 1)], nm_hi_s, 110)
            plan.do("vector", lambda e, b: e.tensor_tensor(nm_hl[:, :, :, 1, :], mx, nm_hl[:, :, :, 0, :].bitcast(F32), ALU.subtract),
                    [(nm_hi_s, half + 1)], nm_lo_s, 150)
            use_m = ring_s.take()

            def emit(e, b):
                for t in tiles:
                    last = e.transpose(use_m["bank"][0:2 * HS, t * P:(t + 1) * P],
                                       nm_hl[:, t, :, :, :].rearrange("p a c j -> p (a c j)").bitcast(F32), ident[:, :])
                return last
            plan.do("tensor", emit, [(nm_lo_s, half + 1), lambda: ring_s.before(use_m)], mt_tr, 430)
            use_m["free"] = (mt_s, plan.do("vector", lambda e, b: e.tensor_copy(m_t[:, :], use_m["bank"][0:2 * HS, :]),
                                           [(mt_tr, half + 1), before(max_in, 2 * half + 2, 2)], mt_s))
            for a in range(2):
                r0 = 64 * a + MROW
                plan.do("sync", lambda e, b, r0=r0, a=a: e.dma_start(
                    q_st[r0:r0 + 2, half, :, :].bitcast(F32), m_t[a * HS:(a + 1) * HS, :].bitcast(F32)),
                    [(mt_s, half + 1)] if a == 0 else [], max_in)

        for half in range(2):
            queries_keys(A1[half], half)
            if half == 0:
                values(A1[half])
            split_values(A1[half], half)
            row_maxima(A1[half], half)
        A1[1].do("gpsimd", lambda e, b: e.tensor_tensor(
            hr[:, :, :], h[:, :, :], row_o[:, :].rearrange("p (o c) -> p o c", o=1).broadcast_to([P, NT, D]), ALU.add),
            [(hfull, None), (x1_s, None, 1)], h_row, 2300)

        def scores_t(plan, hd):
            half, a, j = place(hd)
            slot = hd % NP
            for k2 in range(NT // 2):
                use = ring_t.take()

                def emit(e, b, use=use, k2=k2):
                    for kt in (2 * k2, 2 * k2 + 1):
                        n = min(2 * P, L - kt * P)
                        c0 = (kt % 2) * 2 * P
                        last = e.matmul(use["bank"][:, c0:c0 + n], k_st[:, half, a, j, kt * P:(kt + 1) * P],
                                        q_st[:, half, j, kt * P:kt * P + n], start=True, stop=True)
                    return last
                plan.do("tensor", emit, ([(max_in, 2 * half + 2)] if hd % HS == 0 and k2 == 0 else []) + [lambda use=use: ring_t.before(use)],
                        st_mm, 218 if k2 == 0 else 165)
                c0, n = k2 * 4 * P, min(4 * P, PW - k2 * 4 * P)
                m = plan.do("scalar", lambda e, b, use=use, c0=c0, n=n: e.activation(
                    p32[slot][:, c0:c0 + n], use["bank"][:, 0:n], ACT.Exp, scale=SCALE),
                    [(st_mm, 2 * hd + k2 + 1), low_of(hd - NP)], exp_s, 480 if k2 == 0 else 370, table="exp")
                use["free"] = (exp_s, m)
            plan.do("gpsimd", lambda e, b: e.affine_select(
                out=blocks(p32[slot], 0, NT), in_=blocks(p32[slot], 0, NT), compare_op=ALU.is_ge, fill=0.0, base=0,
                pattern=[[0, NT], [1, P]], channel_multiplier=-1), [(exp_s, 2 * hd + 2)], sel_s, 580, gate=tick_p)
            plan.do("gpsimd", lambda e, b: e.affine_select(
                out=blocks(p32[slot], 1, NT - 1), in_=blocks(p32[slot], 1, NT - 1), compare_op=ALU.is_ge, fill=0.0, base=0,
                pattern=[[0, NT - 1], [-1, P]], channel_multiplier=1), [], sel_s, 460)

        def split_p(plan, hd):
            slot = hd % NP
            free = (av_mm, hd - NP + 1) if hd >= NP else (av_mm, slot_before(hd) + 1, 1)
            plan.do("scalar", lambda e, b: e.activation(p_hi[slot][:, :], p32[slot][:, 0:PW], ACT.Copy),
                    [(sel_s, 2 * hd + 2), free], ph_s, 840)
            plan.do("gpsimd" if on_pool(hd) else "vector", lambda e, b: e.tensor_tensor(
                p_lo[slot][:, :], p32[slot][:, 0:PW], p_hi[slot][:, :], ALU.subtract),
                [(ph_s, hd + 1), free], pl_g if on_pool(hd) else pl_v, 1840 if on_pool(hd) else 1000)

        def blocks(tile, k, n):
            return tile[:, 0:2 * L].rearrange("p (t c) -> p t c", t=NT)[:, 0:n, k * P:(k + 1) * P]

        def on_pool(hd):
            return hd in LOW_ON_POOL

        def slot_before(hd):
            return max(i for i in range(H) if i % NP == hd % NP)

        def low_of(hd):
            back = 0
            if hd < 0:
                hd, back = slot_before(hd + NP), 1
            return (pl_g if on_pool(hd) else pl_v, sum(on_pool(i) == on_pool(hd) for i in range(hd + 1)), back)

        uses_c = {}

        def context(plan, hd):
            slot, pair, half = hd % NP, hd // 2, hd // HS
            if hd % 2 == 0:
                uses_c[pair] = ring_c.take()
            use = uses_c[pair]

            def emit(e, b):
                for qt in tiles:
                    u = (hd % 2) * NT + qt
                    dst = use["bank"][:, u * VW:(u + 1) * VW]
                    pieces = [(pt[slot], kt, qt - kt) for pt in (p_hi, p_lo) for kt in range(max(qt - 1, 0), qt + 1)]
                    for i, (pt, kt, k) in enumerate(pieces):
                        c0 = kt * 2 * P + k * P
                        last = e.matmul(dst, pt[:, c0:c0 + P], v_sb[:, kt * H + hd, :],
                                        start=(i == 0), stop=(i == len(pieces) - 1))
                return last
            w = [low_of(hd)] + ([lambda use=use: ring_c.before(use)] if hd % 2 == 0 else [])
            plan.do("tensor", emit, w + ([(v3_s, half + 1)] if hd % HS == 0 else []), av_mm, 310)
            if hd % 2 == 0:
                return
            s2 = pair % 2
            bank = use["bank"][:, 0:2 * NT * VW].rearrange("p (u w) -> p u w", w=VW)
            plan.do("vector", lambda e, b: e.reciprocal(rsum[:, s2, :], bank[:, :, VW - 1]),
                    [(av_mm, hd + 1), before(ctx_s, pair + 1, 2)], rcp_s, 115)
            n = plan.do("vector", lambda e, b: e.tensor_reduce(
                csum[:, s2, :, :], bank[:, :, 0:3 * HD].rearrange("p u (s d) -> p u d s", s=3), AX.X, ALU.add),
                [], cs_s, 470)
            use["free"] = (cs_s, n)
            dst = cx[:, :, (hd - 1) * HD:(hd + 1) * HD].rearrange("p t (u d) -> p u t d", u=2)
            plan.do("vector", lambda e, b: e.tensor_tensor(
                dst, csum[:, s2, :, :].rearrange("p (u t) d -> p u t d", u=2),
                rsum[:, s2, :].rearrange("p (u t o) -> p u t o", u=2, o=1).broadcast_to([P, 2, NT, HD]), ALU.mult),
                [(cs_s, pair + 1), (ctr, half + 1, 1)], ctx_s, 210)

        for half in range(2):
            h0 = half * HS
            for hd in range(h0, h0 + HS + 2):
                if hd < h0 + HS:
                    scores_t(A2[half], hd)
                if h0 < hd <= h0 + HS:
                    split_p(A2[half], hd - 1)
                if hd >= h0 + 2:
                    context(A2[half], hd - 2)
            use, n = transposes(A2[half], ring_t, lambda t: cx[:, t, :], [(t, half) for t in tiles], [(ctx_s, (half + 1) * HS // 2)], ctr)
            use["free"] = (at2_lo, split(A2[half], ct_hi[:, half, :], ct_lo[:, half, :], use["bank"][:, :],
                                         [(ctr, n), (wo_mm, None, 1)], at2_hi, at2_lo))
        for t2 in range(NT // 2):
            use = token_rows(A2[1], ring_t, t2, ct_hi, ct_lo, wa_hi, wa_lo, 3 * D, [(at2_lo, KC)], wo_mm)
            n = A2[1].do("vector", lambda e, b, t2=t2, use=use: e.tensor_tensor(
                x1[:, 2 * t2:2 * t2 + 2, :], use["bank"][:, :].rearrange("p (t c) -> p t c", t=2),
                hr[:, 2 * t2:2 * t2 + 2, :], ALU.add), [(wo_mm, t2 + 1), (h_row, 1), (x2_s, None, 1)], x1_s)
            use["free"] = (x1_s, n)

        B1.do("sync", lambda e, b: e.dma_start(mod_b[:, :, :], mod_bcast(b, 2)), [(o2_s, None, 1)], modb_in)
        B1.do("sync", lambda e, b: e.dma_start(x2[:, :, :], of_batch(x_t, b)), [(out_s, None, 1)], x_in_b)
        B1.do("vector", lambda e, b: e.tensor_copy(mod_c[:, :], mod_t[:, b, :] if isinstance(b, int) else mod_t[:, bass.ds(b, 1), :].rearrange("p o f -> p (o f)")),
              [(h3_s, None, 1)], modc_s, 80)
        norm_stats(B1, x1, tiles, st_b, mv_b, ve_b, rs_b, st2, mv2, ve2, rs2, lambda t: [(x1_s, None)], (n3_s, None, 1))
        for t in tiles:
            B1.do("vector", lambda e, b, t=t: e.tensor_scalar(
                norm[:, t // 2, t % 2, :], x1[:, t, :], mv_b[:, t, 0:1], rs_b[:, t:t + 1], ALU.subtract, ALU.mult),
                [(rs2, 1), (o3_s, None, 1)], n2_s, 330)
        B1.do("gpsimd", lambda e, b: e.tensor_tensor(
            x1[:, :, :], x1[:, :, :], row_2[:, :].rearrange("p (o c) -> p o c", o=1).broadcast_to([P, NT, D]), ALU.add),
            [(n2_s, NT)], x1_row, 2300)
        for k in range(KC):
            use, n = transposes(B1, ring_b, lambda t: norm[:, t // 2, t % 2, :], [(t, k) for t in tiles], [(n2_s, NT)], tr2)
            use["free"] = (bt1_lo, split(B1, bt_hi[:, k, :], bt_lo[:, k, :], use["bank"][:, :],
                                         [(tr2, n), (vb_mm, None, 1)], bt1_hi, bt1_lo))
        for m in range(MF):
            use = ring_b.take()
            three(B1, use["bank"][:, :], lambda k, m=m: w1_hi[:, k, m * P:(m + 1) * P], lambda k, m=m: w1_lo[:, k, m * P:(m + 1) * P],
                  lambda k: bt_hi[:, k, :], lambda k: bt_lo[:, k, :],
                  [(bt1_lo, KC), lambda use=use: ring_b.before(use)], f1_mm, 216)
            n = B1.do("scalar", lambda e, b, m=m, use=use: e.activation(
                hid[:, :, m, :], use["bank"][:, :].rearrange("p (t n) -> p t n", t=2), ACT.Gelu_apprx_tanh, bias=bias_1[:, m:m + 1]),
                [(f1_mm, m + 1), (o3_s, None, 1)], gelu_s, 570, table="gelu")
            use["free"] = (gelu_s, n)

        def down(t2):
            use = ring_b.take()
            for i in range(2):
                for m0 in range(0, MF, 2):
                    def emit(e, b, i=i, m0=m0):
                        for m in (m0, m0 + 1):
                            last = e.matmul(use["bank"][:, i * D:(i + 1) * D], hid[:, t2, m, i * P:(i + 1) * P],
                                            w2_sb[:, m, :], start=(m == 0), stop=(m == MF - 1))
                        return last
                    B2.do("tensor", emit, [(gelu_s, MF), lambda: ring_b.before(use)] if i == m0 == 0 else [],
                          f2_mm if i and m0 == MF - 2 else None, 864)
            return use

        def second_norm(t2, use):
            ts = slice(2 * t2, 2 * t2 + 2)
            n = B2.do("vector", lambda e, b: e.tensor_tensor(
                x1[:, ts, :], use["bank"][:, :].rearrange("p (t c) -> p t c", t=2), x1[:, ts, :], ALU.add),
                [(f2_mm, t2 + 1), (x1_row, 1)], y_s)
            use["free"] = (y_s, n)
            B2.do("gpsimd", lambda e, b: e.tensor_tensor(
                x1[:, ts, :], x1[:, ts, :], mod_b[:, 0:1, :].broadcast_to([P, 2, D]), ALU.mult),
                [(y_s, t2 + 1), (modb_in, 1)], yg_s)
            B2.do("vector", lambda e, b: e.tensor_tensor(
                x2[:, ts, :], x2[:, ts, :], x1[:, ts, :], ALU.add), [(yg_s, t2 + 1), (x_in_b, 1)], x2_s)
            norm_stats(B2, x2, [2 * t2, 2 * t2 + 1], st_b, mv_b, ve_b, rs_b, st3, mv3, ve3, rs3,
                       lambda t: [(x2_s, t2 + 1), (mv2, t + 1)], (n2_s, NT))
            for t in (2 * t2, 2 * t2 + 1):
                B2.do("vector", lambda e, b, t=t: e.tensor_scalar(
                    norm[:, t // 2, t % 2, :], x2[:, t, :], mv_b[:, t, 0:1], rs_b[:, t:t + 1], ALU.subtract, ALU.mult),
                    [(rs3, t2 + 1), (f2_mm, t2 + 1)], n3_s, 330)

        def mixed(t2):
            ns = slice(2 * t2 * P, (2 * t2 + 2) * P)
            use, n = transposes(B2, ring_b, lambda t: norm[:, t // 2, t % 2, :], [(t, k) for k in range(KC) for t in (2 * t2, 2 * t2 + 1)], [(n3_s, 2 * t2 + 2)], tr3)
            for k in range(KC):
                m = B2.do("scalar", lambda e, b, k=k: e.activation(
                    h3[:, t2, k, 1:2 * P + 1], use["bank"][:, k * 2 * P:(k + 1) * 2 * P], ACT.Identity,
                    bias=mod_c[:, k:k + 1], scale=mod_c[:, KC + k:KC + k + 1]), [(tr3, n), (modc_s, 1), (f2_mm, t2 + 1)], h3_s, 450)
            use["free"] = (h3_s, m)
            if t2 == 0:
                B2.do("vector", lambda e, b: e.memset(h3[:, 0, :, 0:1], 0.0), [(f2_mm, 1)], zcol, 60)
            else:
                B2.do("vector", lambda e, b: e.tensor_copy(h3[:, 1, :, 0:1], h3[:, 0, :, 2 * P:2 * P + 1]),
                      [(h3_s, KC), (f2_mm, 2)], zcol, 70)
            B2.do("gpsimd", lambda e, b: e.tensor_tensor(dif[:, t2, :, :], h3[:, t2, :, 1:2 * P + 1], h3[:, t2, :, 0:2 * P], ALU.subtract),
                  [(h3_s, KC * (t2 + 1)), (zcol, t2 + 1)], dif_s)
            for c_mu, s_x, s_h, s_l, hi, lo, free in ((c_mur, xr_s, xr_h, xr_l, bt_hi, bt_lo, (f1_mm, None)),
                                                      (c_muk, xk_s, xk_h, xk_l, kt_hi, kt_lo, (k_mm, t2 + 1, 1))):
                for k in range(KC):
                    B2.do("vector", lambda e, b, k=k, c_mu=c_mu: e.scalar_tensor_tensor(
                        out=xrk[:, t2, k, :], in0=dif[:, t2, k, :], scalar=col[:, c_mu + k:c_mu + k + 1], in1=h3[:, t2, k, 0:2 * P],
                        op0=ALU.mult, op1=ALU.add), [(dif_s, t2 + 1) if s_x is xr_s else (xr_l, t2 + 1)], s_x, 340)
                split(B2, hi[:, :, ns], lo[:, :, ns], xrk[:, t2, :, :], [(s_x, KC * (t2 + 1)), free], s_h, s_l)

        def receptance(t2):
            use = token_rows(B2, ring_b, t2, bt_hi, bt_lo, wb_hi, wb_lo, 0, [(xr_l, t2 + 1)], r_mm)
            n = B2.do("scalar", lambda e, b: e.activation(tr[:, t2, :], use["bank"][:, :], ACT.Tanh, scale=0.5),
                      [(r_mm, t2 + 1), (f2_mm, t2 + 1)], r_s, table="exp")
            use["free"] = (r_s, n)

        def keys(t2):
            ns = slice(2 * t2 * P, (2 * t2 + 2) * P)
            use = ring_b.take()
            for m in range(KC):
                three(B2, use["bank"][:, m * 2 * P:(m + 1) * 2 * P], lambda k, m=m: wb_hi[:, k, D + m * P:D + (m + 1) * P],
                      lambda k, m=m: wb_lo[:, k, D + m * P:D + (m + 1) * P], lambda k: kt_hi[:, k, ns], lambda k: kt_lo[:, k, ns],
                      [(xk_l, t2 + 1), lambda: ring_b.before(use)] if m == 0 else [], k_mm if m == KC - 1 else None, 109)
            relu = xrk[:, t2, :, :].rearrange("p k n -> p (k n)")
            square = dif[:, t2, :, :].rearrange("p k n -> p (k n)")
            n = B2.do("scalar", lambda e, b: e.activation(relu, use["bank"][:, :], ACT.Relu), [(k_mm, t2 + 1), (xk_l, t2 + 1)], relu_s)
            use["free"] = (relu_s, n)
            B2.do("scalar", lambda e, b: e.activation(square, relu, ACT.Square), [(relu_s, t2 + 1), (xk_s, KC * (t2 + 1))], ksq_s)
            split(B2, bt_hi[:, :, ns], bt_lo[:, :, ns], dif[:, t2, :, :], [(ksq_s, t2 + 1), (r_mm, t2 + 1)], ka_h, ka_l)

        def output(t2):
            ts = slice(2 * t2, 2 * t2 + 2)
            use = token_rows(B2, ring_b, t2, bt_hi, bt_lo, wb_hi, wb_lo, 2 * D, [(ka_l, t2 + 1)], vb_mm)
            n = B2.do("vector", lambda e, b: e.scalar_tensor_tensor(
                out=tr[:, t2, :], in0=tr[:, t2, :], scalar=1.0, in1=use["bank"][:, :], op0=ALU.add, op1=ALU.mult),
                [(vb_mm, t2 + 1), (r_s, t2 + 1)], o1_s)
            use["free"] = (o1_s, n)
            rows = tr[:, t2, :].rearrange("p (t c) -> p t c", c=D)
            B2.do("gpsimd", lambda e, b: e.tensor_tensor(
                rows, rows, mod_b[:, 1:2, :].broadcast_to([P, 2, D]), ALU.mult), [(o1_s, t2 + 1)], o2_s)
            B2.do("vector", lambda e, b: e.tensor_tensor(x2[:, ts, :], x2[:, ts, :], rows, ALU.add),
                  [(o2_s, t2 + 1), (n3_s, 2 * t2 + 2)], o3_s)
            B2.do("sync", lambda e, b: e.dma_start(of_batch(out_t, b)[:, ts, :], x2[:, ts, :]), [(o3_s, t2 + 1)], out_s)

        uses = [down(0), down(1)]
        second_norm(0, uses[0])
        second_norm(1, uses[1])
        mixed(0)
        receptance(0)
        mixed(1)
        keys(0)
        receptance(1)
        keys(1)
        output(0)
        output(1)

        s_col, s_ct, s_rows = sem("s_col"), sem("s_ct"), sem("s_rows")
        s_mod, s_act, s_half, s_pe, s_ones, s_top = (sem(n) for n in ("s_mod", "s_act", "s_half", "s_pe", "s_ones", "s_top"))
        POOL_MASKS, POOL_DONE = 13, 15
        mod_row = x2[0:B, :, :]
        mod_x = mod_b[0:B, :, :]
        ones, cvs = p32[1], p32[2][:, 0:KC * P].rearrange("p (k n) -> p k n", k=KC)
        flat = g[:, :, :].rearrange("p t n -> p (t n)")
        stage = [flat[:, 0:8 * D], flat[:, 8 * D:16 * D]]
        stage_a = stage[0].rearrange("p (k n) -> p k n", k=KC)
        stage_1 = stage[1].rearrange("p (k n) -> p k n", k=KC)
        stage_m = stage[0][:, 0:KC * 3 * D].rearrange("p (k n) -> p k n", k=KC)
        wmod_v = [t.rearrange("p (k a) c -> p k (a c)", k=KC) for t in (x1[:, :, :], w2_sb[:, 0:4, :], w2_sb[:, 4:8, :])]
        pm, pg = psum[7], psum[6]
        pc = psum[7]
        pb, pr = psum[5], psum[4]

        W0 = Plan()
        wa_h, wa_l, b_mm, b_q, cv_s, cvs_s, r_o, row_s = (sig(n) for n in ("wa_h", "wa_l", "b_mm", "b_q", "cv", "cvs", "r_o", "row"))
        landed = {n: sig(n, DMA) for n in ("in_attn", "in_rows", "in_ff1", "in_mix", "in_ff2", "in_mod1", "in_mod2")}

        def load(plan, dst, src, name, cost, waits=()):
            plan.do("sync", lambda e, b: e.dma_start(dst, src), waits, landed[name], cost)

        load(W0, stage_a, w_attn.rearrange("(k p) n -> p k n", p=P), "in_attn", 5000)
        for row, src in ((row_o, bo), (row_2, b2)):
            load(W0, row[:, :], src.rearrange("(o c) -> o c", o=1).broadcast_to([P, D]), "in_rows", 800)
        for k in range(KC):
            W0.do("scalar", lambda e, b, k=k: e.activation(
                wa_hi[:, k, 0:3 * D], stage_a[:, k, 0:3 * D], ACT.Copy, scale=col[:, c_ln1w + k:c_ln1w + k + 1]),
                [(landed["in_attn"], 1)], wa_h, 780)
        W0.do("scalar", lambda e, b: e.activation(wa_hi[:, :, 3 * D:4 * D], stage_a[:, :, 3 * D:4 * D], ACT.Copy), [], wa_h)

        def emit(e, b):
            for m in range(6):
                for k in range(KC):
                    last = e.matmul(pb[:, m:m + 1], stage_a[:, k, m * P:(m + 1) * P], col[:, c_ln1b + k:c_ln1b + k + 1],
                                    start=(k == 0), stop=(k == KC - 1))
            return last
        W0.do("tensor", emit, [(landed["in_attn"], 1)], b_mm, 400)
        W0.do("vector", lambda e, b: e.tensor_tensor(
            bias_q[:, :].rearrange("p (h m) -> p m h", m=2), pb[:, 0:4].rearrange("p (m h) -> p m h", h=2),
            col[:, c_bq:c_bq + 4].rearrange("p (m h) -> p m h", h=2), ALU.add), [(b_mm, 1)], b_q, 70)
        W0.do("vector", lambda e, b: e.tensor_tensor(cv[:, :], pb[:, 4:6], col[:, c_bv:c_bv + KC], ALU.add), [(b_mm, 1)], cv_s, 70)
        W0.do("vector", lambda e, b: e.tensor_copy(cvs, cv[:, :].rearrange("p (k o) -> p k o", o=1).broadcast_to([P, KC, P])),
              [(cv_s, 1)], cvs_s, 200)

        def emit(e, b):
            for k in range(KC):
                last = e.matmul(pr[:, 0:D], cvs[:, k, :], stage_a[:, k, 3 * D:4 * D], start=(k == 0), stop=(k == KC - 1))
            return last
        W0.do("tensor", emit, [(cvs_s, 1)], r_o, 1700)
        for k in range(KC):
            W0.do("vector", lambda e, b, k=k: e.scalar_tensor_tensor(
                out=wa_lo[:, k, 0:3 * D], in0=stage_a[:, k, 0:3 * D], scalar=col[:, c_ln1w + k:c_ln1w + k + 1],
                in1=wa_hi[:, k, 0:3 * D].bitcast(F32), op0=ALU.mult, op1=ALU.subtract), [(wa_h, k + 1)], wa_l, 930)
        W0.do("vector", lambda e, b: e.tensor_tensor(
            wa_lo[:, :, 3 * D:4 * D], stage_a[:, :, 3 * D:4 * D], wa_hi[:, :, 3 * D:4 * D].bitcast(F32), ALU.subtract),
            [(wa_h, KC + 1)], wa_l)
        W0.do("vector", lambda e, b: e.tensor_tensor(row_o[:, :], pr[:, 0:D], row_o[:, :], ALU.add),
              [(r_o, 1), (landed["in_rows"], 2)], row_s, 340)

        WL, W1 = Plan(), Plan()
        g_mm, c_mm, b1_mm, gate_s, modt_s, b1_s, rows_out = (sig(n) for n in ("g_mm", "c_mm", "b1_mm", "gate", "modt", "b1", "rows_out"))
        rows_out.unit = DMA
        w1_h, w1_l, wb_h, wb_l = (sig(n) for n in ("w1_h", "w1_l", "wb_h", "wb_l"))
        for i in (1, 2):
            load(WL, wmod_v[i], w_mod[:, i * 2 * D:(i + 1) * 2 * D].rearrange("(k p) n -> p k n", p=P), f"in_mod{i}", 2700)
        load(WL, stage_1, w_ff1.rearrange("(k p) n -> p k n", p=P), "in_ff1", 5000)
        load(W1, stage_m, w_mix.rearrange("(k p) n -> p k n", p=P), "in_mix", 4000)

        def emit(e, b):
            for i, src in enumerate((wmod_v[1][:, :, 0:D], wmod_v[2][:, :, D:2 * D])):
                for k in range(KC):
                    last = e.matmul(pg[0:B, i * D:(i + 1) * D], sct[:, k, :], src[:, k, :], start=(k == 0), stop=(k == KC - 1))
            return last
        W1.do("tensor", emit, [(landed["in_mod1"], 1), (landed["in_mod2"], 1)], g_mm, 3500)

        def emit(e, b):
            for j, src in enumerate((wmod_v[1][:, :, D:2 * D], wmod_v[2][:, :, 0:D])):
                for m in range(KC):
                    for k in range(KC):
                        u = (2 * j + m) * B
                        last = e.matmul(pc[:, u:u + B], src[:, k, m * P:(m + 1) * P], sct[:, k, :], start=(k == 0), stop=(k == KC - 1))
            return last
        W1.do("tensor", emit, [], c_mm, 300)
        load(W1, w2_sb[:, :, :], w_ff2.rearrange("(m p) n -> p m n", p=P), "in_ff2", 5000, [(c_mm, 1)])

        def emit(e, b):
            for m in range(MF):
                for k in range(KC):
                    last = e.matmul(pc[:, 64 + m:65 + m], stage_1[:, k, m * P:(m + 1) * P], col[:, c_ln2b + k:c_ln2b + k + 1],
                                    start=(k == 0), stop=(k == KC - 1))
            return last
        W1.do("tensor", emit, [(landed["in_ff1"], 1), (modt_s, 2)], b1_mm, 300)
        W1.do("vector", lambda e, b: e.tensor_copy(mod_t[:, :, 0:2], pc[:, 0:2 * B].rearrange("p (m b) -> p b m", b=B)), [(c_mm, 1)], modt_s, 90)
        W1.do("vector", lambda e, b: e.tensor_scalar(
            mod_t[:, :, 2:4], pc[:, 2 * B:4 * B].rearrange("p (m b) -> p b m", b=B), 1.0, None, ALU.add), [], modt_s, 90)
        W1.do("vector", lambda e, b: e.tensor_tensor(bias_1[:, :], pc[:, 64:64 + MF], col[:, c_b1:c_b1 + MF], ALU.add), [(b1_mm, 1)], b1_s, 70)
        n = 0
        for i, factor in enumerate((1.0, 0.5)):
            src, row = pg[0:B, i * D:(i + 1) * D], mod_row[:, 2 + i, :]
            for emit in (lambda e, b, src=src: e.tensor_scalar(mod_x[:, 0, :], src, 0.0, 2.0, ALU.is_ge, ALU.mult),
                         lambda e, b, factor=factor: e.tensor_scalar(mod_x[:, 0, :], mod_x[:, 0, :], -1.0, factor, ALU.add, ALU.mult),
                         lambda e, b, src=src: e.tensor_copy(mod_x[:, 1, :], src),
                         lambda e, b, row=row: e.scalar_tensor_tensor(out=row, in0=mod_x[:, 1, :], scalar=-1.0, in1=mod_x[:, 1, :],
                                                                      op0=ALU.mult, op1=ALU.max),
                         lambda e, b, row=row: e.scalar_tensor_tensor(out=row, in0=row, scalar=0.25, in1=mod_x[:, 0, :],
                                                                      op0=ALU.max, op1=ALU.mult)):
                n = W1.do("vector", emit, [(gate_s, n) if n else (g_mm, 1)], gate_s, 340)
        W1.do("sync", lambda e, b: e.dma_start(scratch[:, 2:4, :], mod_row[:, 2:4, :]), [(gate_s, n)], rows_out)
        for k in range(KC):
            W1.do("scalar", lambda e, b, k=k: e.activation(
                w1_hi[:, k, :], stage_1[:, k, :], ACT.Copy, scale=col[:, c_ln2w + k:c_ln2w + k + 1]), [(landed["in_ff1"], 1)], w1_h, 1030)
            W1.do("vector", lambda e, b, k=k: e.scalar_tensor_tensor(
                out=w1_lo[:, k, :], in0=stage_1[:, k, :], scalar=col[:, c_ln2w + k:c_ln2w + k + 1],
                in1=w1_hi[:, k, :].bitcast(F32), op0=ALU.mult, op1=ALU.subtract), [(w1_h, k + 1)], w1_l, 1200)
        W1.do("scalar", lambda e, b: e.activation(wb_hi[:, :, :], stage_m, ACT.Copy), [(landed["in_mix"], 1)], wb_h, 1370)
        W1.do("vector", lambda e, b: e.tensor_tensor(wb_lo[:, :, :], stage_m, wb_hi[:, :, :].bitcast(F32), ALU.subtract), [(wb_h, 1)], wb_l, 1670)

        def body(b, a0=True, a1=True, a2_first=True, a2_second=True, b1=True, b2=True, w1=False):
            parts = [([(A2[1].steps, -1)] * a2_second + [(A2[0].steps, 0)] * a2_first, "A2"),
                     ([(A1[0].steps, 0), (A1[1].steps, 0)] * a1, "A1"), ([(XA.steps, 1), (A0.steps, 1)] * a0, "A0"),
                     ([(B2.steps, -2)] * b2, "B2"), ([(B1.steps, -1)] * b1, "B1"), ([(W1.steps, 0)] * w1, "W")]
            return order.turn([part for part in parts if part[0]], b)

        order, looped = Order(), 3
        head = order.turn([([(A0.steps, 1)], "A0"), ([(W0.steps, 1), (WL.steps, 1)], "W")], -1)
        turns = [body(0, a2_second=False, b1=False, b2=False, w1=True), body(1, b2=False), body(2), body(looped)]
        for b in range(looped + 1, B - 1):
            order.again(turns[-1], b)
        ends = [body(B - 1, a0=False), body(B, a0=False, a1=False, a2_first=False), order.turn([([(B2.steps, -2)], "B2")], B + 1)]

        def play(eng, name, steps, b):
            for step, offset in steps:
                if step[0] == name:
                    step[1](eng, b + offset if offset else b)

        def batches(eng, name):
            for signal in (row_s, b_q, wa_l):
                wait(eng, signal, None, 0)
            play(eng, name, turns[0], 0)
            for signal in (gate_s, modt_s, b1_s, w1_l, wb_l, rows_out, landed["in_ff2"]):
                wait(eng, signal, None, 0)
            for b in range(1, looped):
                play(eng, name, turns[b], b)
            with eng.Fori(looped, B - 1) as i:
                play(eng, name, turns[-1], i)
            for b, steps in enumerate(ends):
                play(eng, name, steps, B - 1 + b)

        block = ctx.enter_context(nc.Block())

        @block.sync
        def _(e):
            e.dma_start(col[:, :], cols).then_inc(s_col, DMA)
            e.dma_start(ct[:, :, :], c_t.rearrange("(k p) b -> p k b", p=P)).then_inc(s_ct, DMA)
            e.dma_start(wmod_v[0], w_mod[:, 0:2 * D].rearrange("(k p) n -> p k n", p=P)).then_inc(s_mod, DMA)
            play(e, "sync", [(step, 0) for step in XA.steps], 0)
            play(e, "sync", [(step, 0) for step in W0.steps], 0)
            e.wait_ge(s_dve, 3)
            e.dma_start(scratch[:, 0:2, :], mod_row[:, 0:2, :]).then_inc(s_top, DMA)
            e.wait_ge(s_top, DMA)
            play(e, "sync", [(step, 0) for step in A0.steps + WL.steps], 0)
            e.wait_ge(s_pool, POOL_DONE)
            for half in range(2):
                for a in range(2):
                    r0 = 64 * a + MROW
                    e.dma_start(k_st[r0:r0 + 2, half, a, :, :].bitcast(F32), ones[0:4, :]).then_inc(s_ones, DMA)
            e.wait_ge(s_dve, 4)
            e.wait_ge(s_ones, 4 * DMA)
            batches(e, "sync")
            e.wait_ge(out_s.sem, B * out_s.per * DMA)

        @block.gpsimd
        def _(e):
            e.memset(mhalf[:, :], -0.5).then_inc(s_pool, 1)
            e.memset(ident[:, :], 0.0).then_inc(s_pool, 1)
            e.memset(ident_b[:, :], 0.0).then_inc(s_pool, 1)
            e.memset(mask[:, :, :], 0.0).then_inc(s_pool, 1)
            e.memset(ones[:, :], 1.0).then_inc(s_pool, 1)
            e.wait_ge(s_pool, 5)
            e.memset(mask[:, 0, :], NEG).then_inc(s_pool, 1)
            for m in (ident, ident_b):
                e.affine_select(out=m[:, :], in_=m[:, :], compare_op=ALU.not_equal, fill=1.0, base=0,
                                pattern=[[-1, P]], channel_multiplier=1).then_inc(s_pool, 1)
            for i in (1, 3, 5):
                e.affine_select(out=mask[:, i, :], in_=mask[:, i, :], compare_op=ALU.is_ge, fill=NEG, base=0,
                                pattern=[[-1, P]], channel_multiplier=1).then_inc(s_pool, 1)
            for i in (2, 4):
                e.affine_select(out=mask[:, i, :], in_=mask[:, i, :], compare_op=ALU.is_ge, fill=NEG, base=0,
                                pattern=[[1, P]], channel_multiplier=-1).then_inc(s_pool, 1)
            e.wait_ge(s_pool, POOL_MASKS)
            play(e, "gpsimd", head, -1)
            for half in range(2):
                e.memset(k_st[:, half, :, :, :].bitcast(F32), 0.0).then_inc(s_pool, 1)
            batches(e, "gpsimd")

        @block.scalar
        def _(e):
            e.wait_ge(s_ct, DMA)
            e.activation(sct[:, :, :], ct[:, :, :], ACT.Tanh, scale=0.5).then_inc(s_act, 1)
            e.wait_ge(s_col, DMA)
            play(e, "scalar", head, -1)
            batches(e, "scalar")

        @block.tensor
        def _(e):
            e.wait_ge(s_dve, 1)
            e.wait_ge(s_mod, DMA)
            for k in range(KC):
                last = e.matmul(pm[0:B, :], sct[:, k, :], wmod_v[0][:, k, :], start=(k == 0), stop=(k == KC - 1))
            last.then_inc(s_pe, 1)
            e.wait_ge(s_col, DMA)
            e.wait_ge(s_pool, POOL_MASKS)
            e.wait_ge(s_dve, 3)
            play(e, "tensor", head, -1)
            e.wait_ge(s_ones, 4 * DMA)
            batches(e, "tensor")

        @block.vector
        def _(e):
            e.memset(v_sb[:, :, :], 1.0)
            e.wait_ge(s_act, 1)
            e.scalar_tensor_tensor(out=sct[:, :, :], in0=sct[:, :, :], scalar=1.0, in1=ct[:, :, :],
                                   op0=ALU.add, op1=ALU.mult).then_inc(s_half, 1)
            e.wait_ge(s_half, 1)
            e.tensor_scalar(sct[:, :, :], sct[:, :, :], 0.5, None, ALU.mult).then_inc(s_dve, 1)
            e.wait_ge(s_pe, 1)
            e.tensor_scalar(mod_row[:, 0, :], pm[0:B, D:2 * D], 1.0, None, ALU.add).then_inc(s_dve, 1)
            e.tensor_copy(mod_row[:, 1, :], pm[0:B, 0:D]).then_inc(s_dve, 1)
            e.memset(q_st[:, :, :, :].bitcast(F32), 0.0).then_inc(s_dve, 1)
            e.wait_ge(s_col, DMA)
            play(e, "vector", head, -1)
            batches(e, "vector")


def kernel(**inputs):
    import concourse.bacc as bacc
    import numpy as np
    from concourse.bass_utils import run_bass_kernel_spmd

    a = {k: np.asarray(v) for k, v in inputs.items()}
    x = a["L0_attn_x"]
    D, H = x.shape[-1], 16
    order = np.arange(D).reshape(4, H // 4, D // H).transpose(0, 2, 1).reshape(-1)
    halves = lambda v: np.ascontiguousarray(v.reshape(-1, 128).T)
    arrays = {
        "x": x,
        "w_attn": np.concatenate([a["L0_attn_Wq"][:, order], a["L0_attn_Wk"][:, order], a["L0_attn_Wv"], a["L0_attn_Wo"]], axis=1),
        "w_ff1": a["L0_attn_W1"],
        "w_ff2": a["L0_attn_W2"],
        "w_mix": np.concatenate([a["L0_ffn_W_r"].T, a["L0_ffn_W_k"].T, a["L0_ffn_W_v"].T], axis=1),
        "w_mod": a["L0_wmod"],
        "c_t": a["L0_c"].T,
        "cols": np.concatenate([halves(v) for v in (
            a["L0_attn_ln1_w"], a["L0_attn_ln1_b"], a["L0_attn_ln2_w"], a["L0_attn_ln2_b"],
            a["L0_attn_bq"][order], a["L0_attn_bk"][order], a["L0_attn_bv"], a["L0_attn_b1"],
            a["L0_ffn_mu_r"], a["L0_ffn_mu_k"])], axis=1),
        "bo": a["L0_attn_bo"],
        "b2": a["L0_attn_b2"],
    }
    arrays = {k: np.ascontiguousarray(v) for k, v in arrays.items()}
    nc = bacc.Bacc("TRN2", target_bir_lowering=False, num_devices=1, dynamic_dma_scratch_size=1024)
    args = [nc.dram_tensor(k, v.shape, F32, kind="ExternalInput").ap() for k, v in arrays.items()]
    out = nc.dram_tensor("out", x.shape, F32, kind="ExternalOutput").ap()
    adaln_block(nc, *args, out)
    r = run_bass_kernel_spmd(nc, [arrays], core_ids=[0])
    return r.results[0]["out"]
```
